# Optimizing a Trainium2 kernel written in Bass

```python
import numpy as np
import jax
import jax.numpy as jnp

def _softmax(x, axis=-1):
    return jax.nn.softmax(x, axis=axis)
def _gelu(x):
    return jax.nn.gelu(x, approximate=True)
def _silu(x):
    return jax.nn.silu(x)
def _sigmoid(x):
    return jax.nn.sigmoid(x)
def _layernorm(x, axis=-1, eps=1e-5):
    m = jnp.mean(x, axis=axis, keepdims=True)
    v = jnp.var(x, axis=axis, keepdims=True)
    return (x - m) / jnp.sqrt(v + eps)
def _scatter_add(tgt, idx, src, axis=0):
    return tgt.at[idx].add(src)
def _segment_sum(src, seg, n):
    return jax.ops.segment_sum(src, seg, n)

kernel_name = 'mk_dlrm_tower_d1_rec_68a483'

def setup_inputs(seed: int = 0):
    np.random.seed(seed)
    _w = jnp.asarray
    def _rec_inputs():
        import jax
        import jax.numpy as jnp
        _tk = jax.random.key(seed)
        ids = jnp.stack([jax.random.randint(jax.random.fold_in(_tk, 200 + f), (1024,), 0, v, jnp.int32) for f, v in enumerate([10000, 10000, 100000, 1000])], axis=1)
        tbl_0 = 0.05 * jax.random.normal(jax.random.fold_in(_tk, 500 + 0), (10000, 4), jnp.float32)
        tbl_1 = 0.05 * jax.random.normal(jax.random.fold_in(_tk, 500 + 1), (10000, 4), jnp.float32)
        tbl_2 = 0.05 * jax.random.normal(jax.random.fold_in(_tk, 500 + 2), (100000, 4), jnp.float32)
        tbl_3 = 0.05 * jax.random.normal(jax.random.fold_in(_tk, 500 + 3), (1000, 4), jnp.float32)
        _rk = jax.random.fold_in(_tk, 7)
        r_x = 7.22013e-05 + 1.00017 * jax.random.normal(jax.random.fold_in(_rk, 101), (1024, 2048), jnp.float32)
        W_top1 = 0.0197642 * jax.random.normal(jax.random.fold_in(_tk, 801), (2560, 512), jnp.float32)
        W_top2 = 0.0441942 * jax.random.normal(jax.random.fold_in(_tk, 802), (512, 256), jnp.float32)
        W_top3 = 0.0625 * jax.random.normal(jax.random.fold_in(_tk, 803), (256, 1), jnp.float32)
        b_top1 = jnp.zeros((512,), jnp.float32)
        b_top2 = jnp.zeros((256,), jnp.float32)
        return r_x, ids, tbl_0, tbl_1, tbl_2, tbl_3, W_top1, b_top1, W_top2, b_top2, W_top3
    r_x, ids, tbl_0, tbl_1, tbl_2, tbl_3, W_top1, b_top1, W_top2, b_top2, W_top3 = _rec_inputs()
    def _L0_rec_setup():
        import jax, jax.numpy as jnp
        import numpy as np
        B, IN, HID, D, N, OUT = (4096, 2048, 2048, 512, 4, 512)
        H = 8
        HD = D // H

        def _ln(x, g, b):
            m = x.mean(-1, keepdims=True)
            v = ((x - m) ** 2).mean(-1, keepdims=True)
            return (x - m) / jnp.sqrt(v + 1e-05) * g + b
        key = jax.random.key(seed)
        ks = jax.random.split(key, 32)

        def nrm(k, shape, scale=0.02):
            return jax.random.normal(k, shape, jnp.float32) * scale
        inp = {}
        inp['x'] = jax.random.normal(ks[0], (B, IN), jnp.float32)
        inp['strength'] = jax.random.uniform(ks[1], (B, N, N), jnp.float32)
        for t, i in (('er', 2), ('ei', 4)):
            inp[t + '_W1'] = nrm(ks[i], (HID, IN))
            inp[t + '_b1'] = jnp.zeros((HID,), jnp.float32)
            inp[t + '_g1'] = jnp.ones((HID,), jnp.float32)
            inp[t + '_be1'] = jnp.zeros((HID,), jnp.float32)
            inp[t + '_W2'] = nrm(ks[i + 1], (N * D, HID))
            inp[t + '_b2'] = jnp.zeros((N * D,), jnp.float32)
        names = ['Wq_r', 'Wq_i', 'Wk_r', 'Wk_i', 'Wv_r', 'Wv_i', 'Wo_r', 'Wo_i']
        for j, nm in enumerate(names):
            inp[nm] = nrm(ks[6 + j], (D, D))
            inp['b' + nm[1:]] = jnp.zeros((D,), jnp.float32)
        inp['int_Wr'] = jnp.tile(jnp.eye(D, dtype=jnp.float32)[None], (N, 1, 1))
        inp['int_Wi'] = jnp.zeros((N, D, D), jnp.float32)
        inp['meas_Mr'] = nrm(ks[20], (OUT, D), 1.0 / np.sqrt(D))
        inp['meas_Mi'] = nrm(ks[21], (OUT, D), 1.0 / np.sqrt(D))
        inp['post_W'] = nrm(ks[22], (OUT, OUT))
        inp['post_b'] = jnp.zeros((OUT,), jnp.float32)
        inp['post_g'] = jnp.ones((OUT,), jnp.float32)
        inp['post_be'] = jnp.zeros((OUT,), jnp.float32)
        return inp
    _L0_rec_all = _L0_rec_setup()
    _L0_rec_in = {k: v for k, v in _L0_rec_all.items() if k in ('er_W1', 'er_b1', 'er_g1', 'er_be1', 'er_W2', 'er_b2', 'ei_W1', 'ei_b1', 'ei_g1', 'ei_be1', 'ei_W2', 'ei_b2', 'Wq_r', 'bq_r', 'Wq_i', 'bq_i', 'Wk_r', 'bk_r', 'Wk_i', 'bk_i', 'Wv_r', 'bv_r', 'Wv_i', 'bv_i', 'Wo_r', 'bo_r', 'Wo_i', 'bo_i', 'int_Wr', 'int_Wi', 'meas_Mr', 'meas_Mi', 'post_W', 'post_b', 'post_g', 'post_be', )}
    del _L0_rec_all

    return {
        "r_x": r_x,
        "ids": ids,
        "tbl_0": tbl_0,
        "tbl_1": tbl_1,
        "tbl_2": tbl_2,
        "tbl_3": tbl_3,
        "W_top1": W_top1,
        "b_top1": b_top1,
        "W_top2": W_top2,
        "b_top2": b_top2,
        "W_top3": W_top3,
        "L0_rec_er_W1": _L0_rec_in["er_W1"],
        "L0_rec_er_b1": _L0_rec_in["er_b1"],
        "L0_rec_er_g1": _L0_rec_in["er_g1"],
        "L0_rec_er_be1": _L0_rec_in["er_be1"],
        "L0_rec_er_W2": _L0_rec_in["er_W2"],
        "L0_rec_er_b2": _L0_rec_in["er_b2"],
        "L0_rec_ei_W1": _L0_rec_in["ei_W1"],
        "L0_rec_ei_b1": _L0_rec_in["ei_b1"],
        "L0_rec_ei_g1": _L0_rec_in["ei_g1"],
        "L0_rec_ei_be1": _L0_rec_in["ei_be1"],
        "L0_rec_ei_W2": _L0_rec_in["ei_W2"],
        "L0_rec_ei_b2": _L0_rec_in["ei_b2"],
        "L0_rec_Wq_r": _L0_rec_in["Wq_r"],
        "L0_rec_bq_r": _L0_rec_in["bq_r"],
        "L0_rec_Wq_i": _L0_rec_in["Wq_i"],
        "L0_rec_bq_i": _L0_rec_in["bq_i"],
        "L0_rec_Wk_r": _L0_rec_in["Wk_r"],
        "L0_rec_bk_r": _L0_rec_in["bk_r"],
        "L0_rec_Wk_i": _L0_rec_in["Wk_i"],
        "L0_rec_bk_i": _L0_rec_in["bk_i"],
        "L0_rec_Wv_r": _L0_rec_in["Wv_r"],
        "L0_rec_bv_r": _L0_rec_in["bv_r"],
        "L0_rec_Wv_i": _L0_rec_in["Wv_i"],
        "L0_rec_bv_i": _L0_rec_in["bv_i"],
        "L0_rec_Wo_r": _L0_rec_in["Wo_r"],
        "L0_rec_bo_r": _L0_rec_in["bo_r"],
        "L0_rec_Wo_i": _L0_rec_in["Wo_i"],
        "L0_rec_bo_i": _L0_rec_in["bo_i"],
        "L0_rec_int_Wr": _L0_rec_in["int_Wr"],
        "L0_rec_int_Wi": _L0_rec_in["int_Wi"],
        "L0_rec_meas_Mr": _L0_rec_in["meas_Mr"],
        "L0_rec_meas_Mi": _L0_rec_in["meas_Mi"],
        "L0_rec_post_W": _L0_rec_in["post_W"],
        "L0_rec_post_b": _L0_rec_in["post_b"],
        "L0_rec_post_g": _L0_rec_in["post_g"],
        "L0_rec_post_be": _L0_rec_in["post_be"],
    }

def reference(r_x, ids, tbl_0, tbl_1, tbl_2, tbl_3, W_top1, b_top1, W_top2, b_top2, W_top3, L0_rec_er_W1, L0_rec_er_b1, L0_rec_er_g1, L0_rec_er_be1, L0_rec_er_W2, L0_rec_er_b2, L0_rec_ei_W1, L0_rec_ei_b1, L0_rec_ei_g1, L0_rec_ei_be1, L0_rec_ei_W2, L0_rec_ei_b2, L0_rec_Wq_r, L0_rec_bq_r, L0_rec_Wq_i, L0_rec_bq_i, L0_rec_Wk_r, L0_rec_bk_r, L0_rec_Wk_i, L0_rec_bk_i, L0_rec_Wv_r, L0_rec_bv_r, L0_rec_Wv_i, L0_rec_bv_i, L0_rec_Wo_r, L0_rec_bo_r, L0_rec_Wo_i, L0_rec_bo_i, L0_rec_int_Wr, L0_rec_int_Wi, L0_rec_meas_Mr, L0_rec_meas_Mi, L0_rec_post_W, L0_rec_post_b, L0_rec_post_g, L0_rec_post_be):
    import jax
    import jax.numpy as jnp
    def _L0_rec_ref(x, strength, er_W1, er_b1, er_g1, er_be1, er_W2, er_b2, ei_W1, ei_b1, ei_g1, ei_be1, ei_W2, ei_b2, Wq_r, bq_r, Wq_i, bq_i, Wk_r, bk_r, Wk_i, bk_i, Wv_r, bv_r, Wv_i, bv_i, Wo_r, bo_r, Wo_i, bo_i, int_Wr, int_Wi, meas_Mr, meas_Mi, post_W, post_b, post_g, post_be):
        import jax, jax.numpy as jnp
        import numpy as np
        B, IN, HID, D, N, OUT = (4096, 2048, 2048, 512, 4, 512)
        H = 8
        HD = D // H

        def _ln(x, g, b):
            m = x.mean(-1, keepdims=True)
            v = ((x - m) ** 2).mean(-1, keepdims=True)
            return (x - m) / jnp.sqrt(v + 1e-05) * g + b
        Bsz = x.shape[0]

        def enc(W1, b1, g, be, W2, b2):
            h = jax.nn.gelu(_ln(x @ W1.T + b1, g, be), approximate=False)
            return (h @ W2.T + b2).reshape(Bsz, N, D)
        sr = enc(er_W1, er_b1, er_g1, er_be1, er_W2, er_b2)
        si = enc(ei_W1, ei_b1, ei_g1, ei_be1, ei_W2, ei_b2)

        def heads(t):
            return t.reshape(Bsz, N, H, HD).transpose(0, 2, 1, 3)
        qr = heads(sr @ Wq_r.T + bq_r)
        qi = heads(si @ Wq_i.T + bq_i)
        kr = heads(sr @ Wk_r.T + bk_r)
        ki = heads(si @ Wk_i.T + bk_i)
        vr = heads(sr @ Wv_r.T + bv_r)
        vi = heads(si @ Wv_i.T + bv_i)
        ar = jnp.einsum('bhnd,bhmd->bhnm', qr, kr) + jnp.einsum('bhnd,bhmd->bhnm', qi, ki)
        ai = jnp.einsum('bhnd,bhmd->bhnm', qi, kr) - jnp.einsum('bhnd,bhmd->bhnm', qr, ki)
        mag = jnp.sqrt(ar ** 2 + ai ** 2 + 1e-08) * HD ** (-0.5)
        w = jax.nn.softmax(mag, axis=-1)
        out_r = jnp.einsum('bhnm,bhmd->bhnd', w, vr).transpose(0, 2, 1, 3).reshape(Bsz, N, D)
        out_i = jnp.einsum('bhnm,bhmd->bhnd', w, vi).transpose(0, 2, 1, 3).reshape(Bsz, N, D)
        attn_r = out_r @ Wo_r.T + bo_r
        attn_i = out_i @ Wo_i.T + bo_i
        R = jnp.einsum('bnd,ned->bne', attn_r, int_Wr) - jnp.einsum('bnd,ned->bne', attn_i, int_Wi)
        I = jnp.einsum('bnd,ned->bne', attn_r, int_Wi) + jnp.einsum('bnd,ned->bne', attn_i, int_Wr)
        Ri, Ii = (R[:, :, None, :], I[:, :, None, :])
        Rj, Ij = (R[:, None, :, :], I[:, None, :, :])
        phase = jnp.arctan2(Ii * Rj - Ri * Ij, Ri * Rj + Ii * Ij)
        f = jnp.cos(phase) * strength[..., None]
        sup_r = jnp.einsum('bijd,bjd->bd', f, R)
        sup_i = jnp.einsum('bijd,bjd->bd', f, I)
        norm = jnp.sqrt(jnp.sum(sup_r ** 2 + sup_i ** 2, axis=-1, keepdims=True) + 1e-08)
        sup_r = sup_r / norm
        sup_i = sup_i / norm
        mr = sup_r @ meas_Mr.T - sup_i @ meas_Mi.T
        mi = sup_r @ meas_Mi.T + sup_i @ meas_Mr.T
        amp = jnp.sqrt(mr ** 2 + mi ** 2)
        out = jax.nn.gelu(_ln(amp @ post_W.T + post_b, post_g, post_be), approximate=False)
        return out

    e = jnp.stack([tbl_0[ids[:, 0]], tbl_1[ids[:, 1]], tbl_2[ids[:, 2]], tbl_3[ids[:, 3]]], axis=1)
    z = _L0_rec_ref(r_x, e, L0_rec_er_W1, L0_rec_er_b1, L0_rec_er_g1, L0_rec_er_be1, L0_rec_er_W2, L0_rec_er_b2, L0_rec_ei_W1, L0_rec_ei_b1, L0_rec_ei_g1, L0_rec_ei_be1, L0_rec_ei_W2, L0_rec_ei_b2, L0_rec_Wq_r, L0_rec_bq_r, L0_rec_Wq_i, L0_rec_bq_i, L0_rec_Wk_r, L0_rec_bk_r, L0_rec_Wk_i, L0_rec_bk_i, L0_rec_Wv_r, L0_rec_bv_r, L0_rec_Wv_i, L0_rec_bv_i, L0_rec_Wo_r, L0_rec_bo_r, L0_rec_Wo_i, L0_rec_bo_i, L0_rec_int_Wr, L0_rec_int_Wi, L0_rec_meas_Mr, L0_rec_meas_Mi, L0_rec_post_W, L0_rec_post_b, L0_rec_post_g, L0_rec_post_be)
    z = z.reshape(z.shape[0], -1)
    h = jnp.concatenate([z, r_x], axis=1)
    h = jnp.maximum(h @ W_top1 + b_top1, 0.0)
    h = jnp.maximum(h @ W_top2 + b_top2, 0.0)
    y = h @ W_top3
    return y


_drawn_inputs = setup_inputs


def setup_inputs(seed=0):
    import zlib

    import numpy as np

    out = dict(_drawn_inputs(seed))
    spreads = {'b_top1': (0.0, 0.1),
     'b_top2': (0.0, 0.1),
     'L0_rec_er_b1': (0.0, 0.8),
     'L0_rec_er_g1': (1.0, 0.6),
     'L0_rec_er_be1': (0.0, 0.8),
     'L0_rec_er_b2': (0.0, 0.8),
     'L0_rec_ei_b1': (0.0, 0.8),
     'L0_rec_ei_g1': (1.0, 0.6),
     'L0_rec_ei_be1': (0.0, 0.8),
     'L0_rec_ei_b2': (0.0, 0.8),
     'L0_rec_bq_r': (0.0, 0.8),
     'L0_rec_bq_i': (0.0, 0.8),
     'L0_rec_bk_r': (0.0, 0.8),
     'L0_rec_bk_i': (0.0, 0.8),
     'L0_rec_bv_r': (0.0, 0.424),
     'L0_rec_bv_i': (0.0, 0.463),
     'L0_rec_bo_r': (0.0, 0.1),
     'L0_rec_bo_i': (0.0, 0.1),
     'L0_rec_int_Wi': (0.0, 0.1),
     'L0_rec_post_b': (0.0, 0.1),
     'L0_rec_post_g': (1.0, 0.2),
     'L0_rec_post_be': (0.0, 0.1)}
    factors = {'L0_rec_Wq_r': 8.0, 'L0_rec_Wq_i': 8.0, 'L0_rec_Wk_r': 8.0, 'L0_rec_Wk_i': 8.0}
    for name, (base, spread) in spreads.items():
        noise = np.random.default_rng([zlib.crc32(name.encode()), seed]).standard_normal(out[name].shape)
        drawn = base * np.exp(spread * noise) if base else spread * noise
        out[name] = jnp.asarray(drawn.astype(out[name].dtype))
    for name, factor in factors.items():
        out[name] = (out[name] * factor).astype(out[name].dtype)
    return out
```

```python
import concourse.bass as bass
from concourse import mybir
from contextlib import ExitStack

F32 = mybir.dt.float32
F32R = mybir.dt.float32r
I32 = mybir.dt.int32
ACT = mybir.ActivationFunctionType
ALU = mybir.AluOpType
AX = mybir.AxisListType

P = 128
B = 1024
HALVES = 2
HB = B // HALVES
BT = HB // P
IN = 2048
KX = IN // P
HID = 2048
HC = HID // 512
KH = HID // P
D = 512
KD = D // P
N = 4
H = 8
HD = D // H
OC = N * D // P
UNIT = 1024
EPS = 1e-5

U_ENC1 = HC * KX * 512 // UNIT
U_TOP = KX // 2 * 512 // UNIT
U_ENC2 = OC * KH * P // UNIT
U_PASS = U_ENC1 + U_TOP + U_ENC2
U_X = KX * HB // UNIT
X_FROM = U_ENC1 + U_TOP + 8
U_HALF = 2 * U_PASS + U_X
RAW = 4
SPLIT = 2
CREDIT_W = SPLIT
CREDIT_H = 2 * BT

C_G, C_BE, C_B2, C_ENC = 0, KH, 2 * KH, 3 * KH
C_QKVO = 2 * C_ENC
C_TOP1 = C_QKVO + 8 * KD
C_TOP2 = C_TOP1 + KD
C_W3 = C_TOP2 + 2
C_POST = C_W3 + 2
C_ALL = C_POST + 2 * KD

T = B // P
SUB = P // 32
CH = T * KD
Q_R, Q_I, K_R, K_I, V_R, V_I, O_R, O_I = range(8)
SOFT_STEPS = 7
ORDER = (Q_R, K_R, K_I, Q_I)
U_A = U_X + HALVES * U_HALF
U_B = U_A + RAW * T
STEPS = 2 * T
W_COLS = D // 2
ST_A = 16 + HALVES * 2 * (OC + 4) // 2 * 16


def build(nc, x_units, w_units, b1, cols, eye, mask_d, ids, tbls, int_w, meas_w, post_w, post_b, topz_w, top2_w,
          s_T, top_part, at_T, y):
    with ExitStack() as ctx:
        def sb(name, shape, dt, where=ctx):
            return where.enter_context(nc.sbuf_tensor(name, shape, dt))

        def sem(name):
            return ctx.enter_context(nc.semaphore(name))

        ps = ctx.enter_context(nc.psum_tensor("ps", [P, 8, 512], F32))

        colt = sb("colt", [P, C_ALL], F32)
        ident = sb("ident", [P, P], F32)
        ids_t = sb("ids_t", [P, T * N], I32)
        strength = sb("strength", [P, T, N * N], F32)
        strm = ctx.enter_context(ExitStack())
        raw = [sb(f"raw{i}", [P, UNIT], F32, strm) for i in range(RAW)]
        x_hi = sb("x_hi", [P, KX, HB], F32R, strm)
        x_lo = sb("x_lo", [P, KX, HB], F32R, strm)

        enc = ctx.enter_context(ExitStack())
        h = sb("h", [P, BT, HID], F32, enc)
        hT_hi = sb("hT_hi", [P, KH, HB], F32R, enc)
        hT_lo = sb("hT_lo", [P, KH, HB], F32R, enc)
        w_hi = [sb(f"w_hi{i}", [P, UNIT], F32R, enc) for i in range(SPLIT)]
        w_lo = [sb(f"w_lo{i}", [P, UNIT], F32R, enc) for i in range(SPLIT)]
        gel = [sb(f"gel{i}", [P, HB], F32, enc) for i in range(2)]
        stage = [sb(f"stage{i}", [P, HB], F32, enc) for i in range(2)]
        b1row = [sb(f"b1row{i}", [P, 512], F32, enc) for i in range(2)]
        stats = sb("stats", [P, BT, HC, 6], F32, enc)
        meanvar = sb("meanvar", [P, BT, 2], F32, enc)
        std = sb("std", [P, 3, BT], F32, enc)

        enc.close()
        att = ctx.enter_context(ExitStack())
        s_hi = [sb("s_hi0", [P, 2, KD, 512], F32R, att)]
        s_lo = [sb("s_lo0", [P, 2, KD, 512], F32R, att)]
        probs = sb("probs", [P, T, H * SUB, N], F32, att)
        mask = sb("mask", [P, 32], F32, att)
        sco = ctx.enter_context(ExitStack())
        s_hi.append(sb("s_hi1", [P, 2, KD, 512], F32R, sco))
        s_lo.append(sb("s_lo1", [P, 2, KD, 512], F32R, sco))
        q_t = [sb(f"q_t{i}", [P, 2, 2, 512], F32R, sco) for i in range(2)]
        k_t = [sb(f"k_t{i}", [P, 2, 3, 512], F32R, sco) for i in range(2)]
        masked = sb("masked", [P, 4, 512], F32, sco)
        score = [sb(f"score{i}", [P, H * SUB, 2, N], F32, sco) for i in range(2)]
        square = sb("square", [P, H * SUB, 2, N], F32, sco)
        mag = sb("mag", [P, H * SUB, N], F32, sco)
        red = sb("red", [P, 3, H * SUB], F32, sco)

        sco.close()
        val = ctx.enter_context(ExitStack())
        v_t = [sb(f"v_t{i}", [P, 2, H, 2, HD], F32R, val) for i in range(2)]
        o_hi = sb("o_hi", [P, 2, KD, 512], F32R, val)
        o_lo = sb("o_lo", [P, 2, KD, 512], F32R, val)
        wt = [sb(f"wt{i}", [P, 2, H, P], F32R, val) for i in range(2)]
        u_hi = sb("u_hi", [P, T, SUB, H * N], F32R, val)
        u_lo = sb("u_lo", [P, T, SUB, H * N], F32, val)
        out_st = [sb(f"out_st{i}", [P, 512], F32, val) for i in range(4)]
        bv_hi = sb("bv_hi", [P, 2 * KD, 2], F32R, val)
        bv_lo = sb("bv_lo", [P, 2 * KD, 2], F32R, val)
        bo_t = sb("bo_t", [P, 2 * KD], F32, val)

        val.close()
        att.close()
        strm.close()
        sup = ctx.enter_context(ExitStack())
        prod = [sb(f"prod{i}", [P, N, 2, W_COLS], F32, sup) for i in range(2)]
        z_t = [sb(f"z_t{i}", [P, N, 2, D], F32, sup) for i in range(2)]
        sup_T = sb("sup_T", [P, 2, KD, B], F32, sup)
        int_a = sb("int_a", [P, 2, 2, KD, D], F32, sup)
        st_cur = [sb(f"st_cur{i}", [P, N * N], F32, sup) for i in range(2)]
        postb = sb("postb", [P, D], F32, sup)
        norm = sb("norm", [P, 4, 2], F32, sup)
        stats2 = sb("stats2", [P, T, 6], F32, sup)
        mv2 = sb("mv2", [P, T, 2], F32, sup)
        std2 = sb("std2", [P, 3, T], F32, sup)
        int_b = sb("int_b", [P, 2, 2, KD, D], F32, sup)
        at_t = [sb(f"at_t{i}", [P, 3, KD, P], F32, sup) for i in range(2)]
        mag2 = [sb(f"mag2{i}", [P, N, W_COLS], F32, sup) for i in range(2)]
        zero = [sb(f"zero{i}", [P, N, W_COLS], F32, sup) for i in range(2)]
        acc = sb("acc", [P, N, 2, W_COLS], F32, sup)
        gsum = sb("gsum", [P, N, W_COLS], F32, sup)
        sup_t = [sb(f"sup_t{i}", [P, 2, D], F32, sup) for i in range(2)]
        junk = sb("junk", [P, 2, D], F32, sup)
        meas = int_a[:, 0, :, :, :]
        meas_neg = int_a[:, 1, 0, :, :]
        post_wt = int_a[:, 1, 1, :, :]
        topz = int_b[:, 0, 0, :, :]
        sq = int_b[:, 0, 1, :, :]
        amp_T = int_b[:, 1, :, :, :]
        row_t = [at_t[t % 2][:, t // 2, :, :].rearrange("p k b -> p (k b)") for t in range(BT)]
        flat4 = "p n e d -> p (n e d)"
        z_out = [prod[hf][:, :, :, :].rearrange(flat4).rearrange("p (k b) -> p k b", k=KD) for hf in range(2)]
        part = z_t
        h1_T = acc[:, :, :, :].rearrange(flat4).rearrange("p (k b) -> p k b", k=KD)
        h2_T = gsum[:, :, :].rearrange("p n d -> p (n d)").rearrange("p (k b) -> p k b", k=2)
        top2_wt = mag2[0]
        y_row = mag2[1][0:1, :, :].rearrange("p n d -> p (n d)")

        consts_in = sem("consts_in")
        raw_in = [sem(f"raw_in{i}") for i in range(RAW)]
        hi_done = sem("hi_done")
        split_done = sem("split_done")
        w_used = sem("w_used")
        b1_in = [sem(f"b1_in{i}") for i in range(2)]
        h_evac = sem("h_evac")
        bn_done = sem("bn_done")
        var_done = sem("var_done")
        std_done = sem("std_done")
        norm_step = sem("norm_step")
        ln_done = sem("ln_done")
        tr_done = sem("tr_done")
        gelu_done = sem("gelu_done")
        hT_high = sem("hT_high")
        hT_done = sem("hT_done")
        top_evac = sem("top_evac")
        s_evac = sem("s_evac")
        st_out = [sem(f"st_out{i}") for i in range(2)]

        s_high = sem("s_high")
        qk_mm = sem("qk_mm")
        qk_high = sem("qk_high")
        qk_low = sem("qk_low")
        neg_done = sem("neg_done")
        sc_mm = sem("sc_mm")
        sc_masked = sem("sc_masked")
        sc_sum = sem("sc_sum")
        soft = sem("soft")
        mag_done = sem("mag_done")
        exp_done = sem("exp_done")
        mask_in = sem("mask_in")
        u_moved = sem("u_moved")
        bv_high = sem("bv_high")
        bv_low = sem("bv_low")
        bias_mm = sem("bias_mm")
        bias_done = sem("bias_done")
        v_mm = sem("v_mm")
        v_high = sem("v_high")
        v_low = sem("v_low")
        wt_high = sem("wt_high")
        wt_done = sem("wt_done")
        av_mm = sem("av_mm")
        o_high = sem("o_high")
        o_low = sem("o_low")
        wo_mm = sem("wo_mm")
        wo_evac = sem("wo_evac")
        at_out = [sem(f"at_out{i}") for i in range(4)]

        ids_in = sem("ids_in")
        emb_in = sem("emb_in")
        int_in = [sem(f"int_in{i}") for i in range(N)]
        at_in = [sem(f"at_in{i}") for i in range(2)]
        neg2 = sem("neg2")
        z_mm = sem("z_mm")
        z_evac = sem("z_evac")
        cur = sem("cur")
        sq_done = sem("sq_done")
        m_step = sem("m_step")
        rt_done = sem("rt_done")
        rc_done = sem("rc_done")
        u_done = sem("u_done")
        a_step = sem("a_step")
        ua_done = sem("ua_done")
        g_done = sem("g_done")
        g_step = sem("g_step")
        zg_done = sem("zg_done")
        t_step = sem("t_step")
        nrm_sq = sem("nrm_sq")
        nrm_a = sem("nrm_a")
        nrm_rt = sem("nrm_rt")
        nrm_b = sem("nrm_b")
        st_mm = sem("st_mm")
        st_evac = sem("st_evac")
        fin_in = {x: sem(f"{x}_in") for x in ("meas", "post", "postb", "topz", "part0", "part1", "top2")}
        neg3 = sem("neg3")
        me_mm = sem("me_mm")
        me_sq = sem("me_sq")
        me_sum = sem("me_sum")
        amp = sem("amp")
        row_mm = sem("row_mm")
        row_in = sem("row_in")
        row_bn = sem("row_bn")
        row_mv = sem("row_mv")
        row_var = sem("row_var")
        row_std = sem("row_std")
        row_rstd = sem("row_rstd")
        row_ln = sem("row_ln")
        row_tr = sem("row_tr")
        z_gelu = sem("z_gelu")
        part_sum = sem("part_sum")
        t1_mm = sem("t1_mm")
        t1_sum = sem("t1_sum")
        t1_relu = sem("t1_relu")
        t2_mm = sem("t2_mm")
        t2_relu = sem("t2_relu")
        y_mm = sem("y_mm")
        y_done = sem("y_done")
        y_out = sem("y_out")

        def col(base, n=1):
            return colt[:, base:base + n]

        def mm3(pe, out, lh, ll, rh, rl, start, stop):
            pe.matmul(out, ll, rh, start=start, stop=False)
            pe.matmul(out, lh, rl, start=False, stop=False)
            return pe.matmul(out, lh, rh, start=False, stop=stop)

        def stream_before(half, e):
            return U_X + half * U_HALF + e * U_PASS

        def stream_pos(half, e, u, late=False):
            extra = 0
            if e == 1 and late:
                extra = U_X
            elif e == 1 and isinstance(u, int):
                extra = min(max(u - X_FROM, 0), U_X)
            return stream_before(half, e) + u + extra

        block = ctx.enter_context(nc.Block())

        @block.sync
        def _(sp):
            sp.dma_start(colt[:, :], cols).then_inc(consts_in, 16)
            sp.dma_start(ident[:, :], eye).then_inc(consts_in, 16)
            sp.dma_start(ids_t[:, :], ids).then_inc(ids_in, 16)
            for u in range(U_X):
                if u >= RAW:
                    sp.wait_ge(split_done, u - RAW + 1)
                sp.dma_start(raw[u % RAW][:, :], x_units[0, u]).then_inc(raw_in[u % RAW], 16)

            def load(pos, src, slot):
                sp.wait_ge(split_done, pos - RAW + 1)
                sp.dma_start(raw[slot][:, :], src).then_inc(raw_in[slot], 16)

            with sp.Fori(0, HALVES) as half:
                for e in range(2):
                    fixed = X_FROM
                    with sp.Fori(0, fixed // RAW) as g:
                        for s in range(RAW):
                            load(stream_before(half, e) + g * RAW + s, w_units[e, g * RAW + s], s)
                    for u in range(fixed, fixed + 8):
                        pos = stream_pos(half, e, u)
                        k = (U_X + e * U_PASS + u + (u - fixed if e else 0)) % RAW
                        load(pos, w_units[e, u], k)
                        if e:
                            load(pos + 1, x_units[half + 1, u - fixed], (k + 1) % RAW)
                    with sp.Fori(fixed // RAW + 2, U_PASS // RAW) as g:
                        for s in range(RAW):
                            load(stream_before(half, e) + (U_X if e else 0) + g * RAW + s,
                                 w_units[e, g * RAW + s], s)

            def load_s(t):
                for u in range(RAW):
                    e, g = u // 2, u % 2
                    load(t * RAW + U_A + u,
                         s_T[e, bass.ds(t, 1), :, 2 * g:2 * g + 2, :, :].rearrange("o p k n b -> (o p) (k n b)"), u)

            for i in range(2):
                sp.wait_ge(st_out[i], 16 + 320)
            load_s(0)
            for i in range(2):
                sp.wait_ge(st_out[i], ST_A)
            sp.wait_ge(tr_done, 4 * KH)
            sp.dma_start(mask[:, :], mask_d).then_inc(mask_in, 16)
            with sp.Fori(1, T) as t:
                load_s(t)

            def load_sv(t, pos):
                for u in range(RAW):
                    e, g = u // 2, u % 2
                    load(pos + u, s_T[e, bass.ds(t, 1), :, 2 * g:2 * g + 2, :, :].rearrange("o p k n b -> (o p) (k n b)"), u)

            def store_at(t):
                for j in range(8):
                    sp.wait_ge(wo_evac, t * 8 + j + 1)
                    sp.dma_start(at_T[bass.ds(t, 1), :, :, j // 4, j % 4, :].rearrange("o n p b -> p (o n) b"),
                                 out_st[j % 4][:, :].rearrange("p (n b) -> p n b", n=N)).then_inc(at_out[j % 4], 16)

            load_sv(0, U_B)
            for u in range(U_X):
                load(U_B + RAW + u, x_units[3, u], u % RAW)
            load_sv(1, U_B + U_X + RAW)
            with sp.Fori(0, T - 2) as t:
                store_at(t)
                load_sv(t + 2, U_B + U_X + 2 * RAW + t * RAW)
            store_at(T - 2)
            store_at(T - 1)
            for i in range(4):
                sp.wait_ge(at_out[i], 16 + 2 * T * 16)

            def load_at(t, n):
                s = n % 2
                if not (isinstance(t, int) and t == 0 and n < 2):
                    sp.wait_ge(z_mm, t * 8 + 2 * n - 2)
                sp.dma_start(at_t[s][:, 0:2, :, :].rearrange("p e k b -> p (e k b)"),
                             at_T[bass.ds(t, 1), n, :, :, :, :].rearrange("o p e k b -> (o p) (e k b)")).then_inc(at_in[s], 16)

            sp.wait_ge(wo_mm, 8 * T)
            sp.wait_ge(av_mm, 2 + SUB * T)
            for n in range(2):
                sp.dma_start(int_a[:, n, :, :, :].rearrange("p e k d -> p (e k d)"), int_w[n]).then_inc(int_in[n], 16)
                load_at(0, n)
            for n in range(2, 4):
                sp.dma_start(int_b[:, n - 2, :, :, :].rearrange("p e k d -> p (e k d)"), int_w[n]).then_inc(int_in[n], 16)
            for n in range(2, 4):
                load_at(0, n)
            with sp.Fori(1, T) as t:
                for n in range(N):
                    load_at(t, n)

            sp.dma_start(postb[:, :], post_b.to_broadcast((P, D))).then_inc(fin_in["postb"], 16)
            sp.wait_ge(z_mm, 8 * T - 6)
            sp.dma_start(meas.rearrange("p e k d -> p (e k d)"), meas_w).then_inc(fin_in["meas"], 16)
            sp.wait_ge(z_mm, 8 * T - 4)
            sp.dma_start(post_wt.rearrange("p k d -> p (k d)"), post_w).then_inc(fin_in["post"], 16)
            sp.wait_ge(z_mm, 8 * T - 2)
            sp.dma_start(topz.rearrange("p k d -> p (k d)"), topz_w).then_inc(fin_in["topz"], 16)
            for hf in range(HALVES):
                sp.wait_ge(t_step, 4 * (T - 1 + hf))
                for e in range(2):
                    sp.dma_start(part[hf][:, :, e, :], top_part[e, :, :, hf * HB:hf * HB + HB].rearrange("c p b -> p c b")
                                 ).then_inc(fin_in[f"part{hf}"], 16)
            sp.dma_start(top2_wt[:, :, :].rearrange("p k d -> p (k d)"), top2_w).then_inc(fin_in["top2"], 16)
            sp.wait_ge(y_done, 2)
            sp.dma_start(y, y_row).then_inc(y_out, 16)
            sp.wait_ge(y_out, 16)

        @block.scalar
        def _(act):
            for s in range(2):
                act.sem_inc(st_out[s], 16)
            for u in range(U_X):
                act.wait_ge(raw_in[u % RAW], (u // RAW + 1) * 16)
                act.activation(x_hi[:, 2 * u:2 * u + 2, :], raw[u % RAW][:, :].rearrange("p (k b) -> p k b", k=2),
                               ACT.Identity).then_inc(hi_done, 1)

            def landed(pos, slot):
                act.wait_ge(raw_in[slot], (pos - slot) * 4 + 16)

            def high(half, e, u, static, late=False):
                pos = stream_pos(half, e, u, late)
                landed(pos, static % RAW)
                act.wait_ge(w_used, half * 2 * U_PASS + e * U_PASS + u - SPLIT + 1 + CREDIT_W)
                act.activation(w_hi[u_slot(u, static)][:, :], raw[static % RAW][:, :], ACT.Identity).then_inc(hi_done, 1)

            def u_slot(u, static):
                return static % SPLIT

            act.wait_ge(consts_in, 32)
            with act.Fori(0, HALVES) as half:
                for e in range(2):
                    def it(n):
                        return half * (2 * n) + e * n

                    with act.Fori(0, HC // 2) as hp:
                        for par in range(2):
                            act.wait_ge(h_evac, it(4 * HC) + hp * 8 + par * 4 + 4)
                            act.dma_start(b1row[par][:, :],
                                          b1[e, bass.ds(hp * 1024 + par * 512, 512)].rearrange("(a n) -> a n", a=1).to_broadcast((P, 512))
                                          ).then_inc(b1_in[par], 16)
                            for j in range(8):
                                high(half, e, hp * 16 + par * 8 + j, par * 8 + j)
                    u0 = U_ENC1
                    for j in range(3):
                        high(half, e, u0 + j, u0 + j)
                    act.wait_ge(var_done, it(1) + 1)
                    act.activation(std[:, 1, :], std[:, 0, :], ACT.Sqrt).then_inc(std_done, 1)
                    high(half, e, u0 + 3, u0 + 3)
                    u2 = U_ENC1 + U_TOP
                    high(half, e, u2, u2)
                    high(half, e, u2 + 1, u2 + 1)

                    def store_top(c):
                        act.wait_ge(top_evac, it(4) + c + 1)
                        act.dma_start(top_part[e, c, :, bass.ds(half * HB, HB)], stage[c % 2][:, :]).then_inc(st_out[c % 2], 16)

                    for k in range(KH):
                        act.wait_ge(tr_done, it(KH) + k + 1)
                        if k >= 2:
                            act.wait_ge(hT_done, it(KH) + k - 1)
                        act.activation(gel[k % 2][:, :], ps[:, 4 + k % 4, :], ACT.Gelu,
                                       scale=col(e * C_ENC + C_G + k), bias=col(e * C_ENC + C_BE + k)).then_inc(gelu_done, 1)
                        if k in (2, 4, 6, 8):
                            store_top(k // 2 - 1)
                        if k == 11:
                            high(half, e, u2 + 2, u2 + 2)
                    high(half, e, u2 + 3, u2 + 3)

                    def store_s(oc, n, kd):
                        act.wait_ge(s_evac, it(OC) + oc + 2)
                        dst = s_T[e, bass.ds(half * BT, BT), :, kd, n, :].rearrange("t p b -> p t b")
                        act.dma_start(dst, stage[kd % 2][:, :].rearrange("p (t b) -> p t b", t=BT)).then_inc(st_out[kd % 2], 16)

                    store_s(0, 0, 0)
                    for oc in range(1, 8):
                        for v in range(2):
                            u = u2 + 2 * oc + 2 + v
                            if oc < 7:
                                st = (U_X + e * U_PASS + u + (min(max(u - u2 - 8, 0), 8) if e else 0))
                                pos = stream_pos(half, e, u)
                                landed(pos, st % RAW)
                                act.wait_ge(w_used, half * 2 * U_PASS + e * U_PASS + u - SPLIT + 1 + CREDIT_W)
                                act.activation(w_hi[u % SPLIT][:, :], raw[st % RAW][:, :], ACT.Identity).then_inc(hi_done, 1)
                                if e and u - u2 >= 8:
                                    xu = u - u2 - 8
                                    landed(pos + 1, (st + 1) % RAW)
                                    act.activation(x_hi[:, 2 * xu:2 * xu + 2, :],
                                                   raw[(st + 1) % RAW][:, :].rearrange("p (k b) -> p k b", k=2),
                                                   ACT.Identity).then_inc(hi_done, 1)
                        if oc < 7:
                            store_s(oc, oc // 4, oc % 4)
                    with act.Fori(2, OC // 4) as og:
                        for q in range(4):
                            for v in range(2):
                                high(half, e, u2 + og * 8 + 2 * q + v, u2 + 2 * q + v, True)
                            if q == 0:
                                store_s_dyn = (og * 4 - 1, og - 1, 3)
                            else:
                                store_s_dyn = (og * 4 + q - 1, og, q - 1)
                            store_s(*store_s_dyn)
                    store_s(OC - 1, N - 1, KD - 1)

            def high_s(t, slot):
                for e in range(2):
                    for kd in range(KD):
                        u = e * 2 + kd // 2
                        if kd % 2 == 0:
                            act.wait_ge(raw_in[u], t * 16 + (U_A // RAW + 1) * 16)
                            act.wait_ge(qk_mm, t * 16 - 16) if not (isinstance(t, int) and t < 2) else None
                        src = raw[u][:, kd % 2 * 512:kd % 2 * 512 + 512].rearrange("p (n s b) -> p s n b", n=N, s=SUB)
                        act.activation(s_hi[slot][:, e, kd, :].rearrange("p (s n b) -> p s n b", n=N, s=SUB), src,
                                       ACT.Identity).then_inc(s_high, 1)

            def high_qk(g, c, slot):
                act.wait_ge(sc_mm, 4 * g + 4)
                for a, m in enumerate(ORDER):
                    act.wait_ge(qk_mm, 4 * g + a + 1)
                    dst = q_t[slot][:, 0, int(m == Q_I), :] if m in (Q_R, Q_I) else k_t[slot][:, 0, int(m == K_R), :]
                    act.activation(dst, ps[:, a, :], ACT.Identity, bias=col(C_QKVO + m * KD + c)).then_inc(qk_high, 1)
                act.wait_ge(qk_low, 4 * g + 4 + 3)
                act.activation(k_t[slot][:, :, 2, :], k_t[slot][:, :, 0, :].bitcast(F32), ACT.Copy, scale=-1.0).then_inc(neg_done, 1)

            def score_tile(t, first=False, last=False):
                par = t[1]
                t = t[0]
                for c in range(KD):
                    high_qk(t * 4 + c, c, c % 2)
                    if c == 1:
                        high_s(t + 1, 1 - par)
                    if not first and c == 1:
                        act.wait_ge(soft, t * SOFT_STEPS - SOFT_STEPS + 2)
                        act.activation(mag[:, :, :], square[:, :, 0, :], ACT.Sqrt).then_inc(mag_done, 1)
                    if not first and c == 2:
                        act.wait_ge(soft, t * SOFT_STEPS - SOFT_STEPS + 4)
                        act.activation(mag[:, :, :], mag[:, :, :], ACT.Exp, scale=HD ** -0.5).then_inc(exp_done, 1)

            act.wait_ge(tr_done, 4 * KH)
            act.wait_ge(w_used, CREDIT_W + 4 * U_PASS)
            high_s(0, 0)
            score_tile((0, 0), first=True)
            with act.Fori(0, 3) as i:
                score_tile((2 * i + 1, 1))
                score_tile((2 * i + 2, 0))
            score_tile((7, 1), last=True)
            for s in range(4):
                act.sem_inc(at_out[s], 16)
            act.activation(bv_hi[:, :, 0], col(C_QKVO + V_R * KD, 2 * KD), ACT.Identity).then_inc(bv_high, 1)
            act.activation(bv_hi[:, :, 1], col(C_QKVO + V_R * KD, 2 * KD), ACT.Identity).then_inc(bv_high, 1)

            def high_vo(u):
                act.wait_ge(qk_mm, 4 * CH)
                act.wait_ge(raw_in[u % RAW], ((U_B + RAW + u) // RAW + 1) * 16)
                act.activation(x_hi[:, 2 * u:2 * u + 2, :], raw[u % RAW][:, :].rearrange("p (k b) -> p k b", k=2),
                               ACT.Identity).then_inc(hi_done, 1)

            for u in range(4):
                high_vo(u)
            act.wait_ge(soft, T * SOFT_STEPS - SOFT_STEPS + 2)
            act.activation(mag[:, :, :], square[:, :, 0, :], ACT.Sqrt).then_inc(mag_done, 1)
            act.wait_ge(soft, T * SOFT_STEPS - SOFT_STEPS + 4)
            act.activation(mag[:, :, :], mag[:, :, :], ACT.Exp, scale=HD ** -0.5).then_inc(exp_done, 1)
            for u in range(4, U_X):
                high_vo(u)

            def high_sv(t, e, kd):
                u = e * 2 + kd // 2
                if kd % 2 == 0:
                    act.wait_ge(raw_in[u], t * 16 + ((U_B + U_X) // RAW + 1) * 16)
                src = raw[u][:, kd % 2 * 512:kd % 2 * 512 + 512].rearrange("p (n s b) -> p s n b", n=N, s=SUB)
                act.activation(s_hi[0][:, e, kd, :].rearrange("p (s n b) -> p s n b", n=N, s=SUB), src,
                               ACT.Identity).then_inc(s_high, 1)

            def high_v(q, sub):
                for e in range(2):
                    act.wait_ge(v_mm, 2 * q + e + 1)
                    act.activation(v_t[sub % 2][:, 0, :, e, :], ps[:, sub % 2 * 2 + e, :].rearrange("p (h d) -> p h d", h=H),
                                   ACT.Identity).then_inc(v_high, 1)

            def high_o(q, sub):
                act.wait_ge(av_mm, 2 + q + 1)
                b = 4 + sub % 2 * 2
                for e in range(2):
                    for hh in range(2):
                        act.activation(o_hi[HD * hh:HD * hh + HD, e, :, sub * P:sub * P + P],
                                       ps[HD * e:HD * e + HD, b:b + 2, :].rearrange("p k (c z q) -> p (k c) z q", c=2, z=2)[:, :, hh, :],
                                       ACT.Identity).then_inc(o_high, 1)

            def value_tile(t, last=False):
                for sub in range(SUB):
                    high_v(t * 4 + sub, sub)
                    if sub:
                        high_o(t * 4 + sub - 1, sub - 1)
                high_o(t * 4 + 3, 3)
                for j in range(8):
                    act.wait_ge(wo_mm, t * 8 + j + 1)
                    act.wait_ge(at_out[j % 4], t * 32 + j // 4 * 16 + 16)
                    if isinstance(t, int) and t == 0 and j == 0:
                        act.wait_ge(bias_done, 1)
                    act.activation(out_st[j % 4][:, :].rearrange("p (n s b) -> p s n b", n=N, s=SUB),
                                   ps[:, j % 4, :].rearrange("p (s n b) -> p s n b", n=N, s=SUB), ACT.Identity,
                                   bias=bo_t[:, j:j + 1]).then_inc(wo_evac, 1)
                    if not last:
                        if j == 0:
                            act.wait_ge(v_mm, t * 8 + 8)
                        high_sv(t + 1, j // 4, j % 4)

            value_tile(0)
            with act.Fori(1, T - 1) as t:
                value_tile(t)
            value_tile(T - 1, last=True)

            def half(f):
                return slice(f % 2 * W_COLS, f % 2 * W_COLS + W_COLS)

            def squares(f, q, t):
                act.wait_ge(z_evac, t * 8 + 8)
                if not (isinstance(f, int) and f < 2):
                    act.wait_ge(t_step, f * 2 - 2)
                act.activation(prod[q % 2][:, :, :, :].rearrange("p n e d -> p (n e) d"),
                               z_t[q // 2 % 2][:, :, :, half(q)].rearrange("p n e d -> p (n e) d"), ACT.Square).then_inc(sq_done, 1)

            def roots(f, q):
                act.wait_ge(m_step, f * 3 + 3)
                act.activation(mag2[q % 2][:, :, :], mag2[q % 2][:, :, :], ACT.Sqrt).then_inc(rt_done, 1)

            def norm_squares(t, q):
                act.wait_ge(t_step, t * 4 + 4)
                if not (isinstance(t, int) and t == 0):
                    act.wait_ge(nrm_sq, t)
                act.activation(junk[:, :, :], sup_t[q // 2 % 2][:, :, :], ACT.Square, accum_out=norm[:, 0, q // 2 % 2:q // 2 % 2 + 1]).then_inc(nrm_sq, 1)

            def norm_root(t, q):
                act.wait_ge(nrm_a, t + 1)
                act.activation(norm[:, 2, q // 2 % 2:q // 2 % 2 + 1], norm[:, 1, q // 2 % 2:q // 2 % 2 + 1], ACT.Sqrt).then_inc(nrm_rt, 1)

            def evac_sup(t):
                for e in range(2):
                    act.wait_ge(st_mm, t * 2 + e + 1)
                    act.activation(sup_T[:, e, :, bass.ds(t * P, P)], ps[:, 6 + e, :].rearrange("p (k b) -> p k b", k=KD),
                                   ACT.Identity).then_inc(st_evac, 1)

            def evac_z(t, par, n):
                for e in range(2):
                    act.wait_ge(z_mm, t * 8 + 2 * n + e + 1)
                    if not (isinstance(t, int) and t < 2):
                        act.wait_ge(t_step, t * 4 - 4)
                    act.activation(z_t[par][:, n, e, :], ps[:, n % 2 * 2 + e, :], ACT.Identity).then_inc(z_evac, 1)

            def negate(t, n):
                act.wait_ge(at_in[n % 2], t * 32 + n // 2 * 16 + 16)
                act.activation(at_t[n % 2][:, 2, :, :], at_t[n % 2][:, 1, :, :], ACT.Copy, scale=-1.0).then_inc(neg2, 1)

            def sup_tile(t, par):
                now = isinstance(t, int)
                q = 2 * (1 - par)
                if not now or t >= 1:
                    squares(2 * t - 2, q, t - 1)
                    roots(2 * t - 2, q)
                negate(t, 1) if not (now and t == 0) else None
                evac_z(t, par, 0)
                negate(t, 2)
                evac_z(t, par, 1)
                if not now or t >= 1:
                    squares(2 * t - 1, q + 1, t - 1)
                if not now or t >= 2:
                    norm_squares(t - 2, 2 * par)
                if not now or t >= 1:
                    roots(2 * t - 1, q + 1)
                if not now or t >= 2:
                    norm_root(t - 2, 2 * par)
                negate(t, 3)
                evac_z(t, par, 2)
                if not (now and t == T - 1):
                    negate(t + 1, 0)
                evac_z(t, par, 3)
                if not now or t >= 2:
                    evac_sup(t - 2)

            negate(0, 0)
            negate(0, 1)
            sup_tile(0, 0)
            sup_tile(1, 1)
            with act.Fori(1, T // 2 - 1) as i:
                sup_tile(2 * i, 0)
                sup_tile(2 * i + 1, 1)
            sup_tile(T - 2, 0)
            sup_tile(T - 1, 1)

            def measured_squares(hf, c):
                g = hf * KD + c
                act.wait_ge(me_mm, g + 1)
                if g >= 2:
                    act.wait_ge(me_sum, g - 1)
                for e in range(2):
                    act.activation(sq[:, c % 2 * 2 + e, :], ps[:, c % 2 * 2 + e, :], ACT.Square).then_inc(me_sq, 1)

            def amplitude(hf, c):
                act.wait_ge(me_sum, hf * KD + c + 1)
                act.activation(amp_T[:, hf, c, :], amp_T[:, hf, c, :], ACT.Sqrt).then_inc(amp, 1)

            def row_root(t):
                act.wait_ge(row_var, t + 1)
                act.activation(std2[:, 1, t:t + 1], std2[:, 0, t:t + 1], ACT.Sqrt).then_inc(row_std, 1)

            def row_gelu(t):
                act.wait_ge(row_tr, t + 1)
                for k in range(KD):
                    act.activation(z_out[t // BT][:, k, t % BT * P:t % BT * P + P], ps[:, 6 + t % 2, k * P:k * P + P], ACT.Gelu,
                                   bias=col(C_POST + KD + k), scale=col(C_POST + k)).then_inc(z_gelu, 1)

            def relu_1(hf):
                for c in range(KD):
                    act.wait_ge(t1_sum, hf * KD + c + 1)
                    act.activation(h1_T[:, c, :], h1_T[:, c, :], ACT.Relu, bias=col(C_TOP1 + c)).then_inc(t1_relu, 1)

            def relu_2(hf):
                for c in range(2):
                    act.wait_ge(t2_mm, hf * 2 + c + 1)
                    act.activation(h2_T[:, c, :], ps[:, 4 + c, :], ACT.Relu, bias=col(C_TOP2 + c)).then_inc(t2_relu, 1)

            def result(hf):
                act.wait_ge(y_mm, hf + 1)
                act.activation(y_row[:, hf * HB:hf * HB + HB], ps[0:1, 6, :], ACT.Identity).then_inc(y_done, 1)

            act.wait_ge(fin_in["meas"], 16)
            act.wait_ge(z_mm, 8 * T - 4)
            act.activation(meas_neg, meas[:, 1, :, :], ACT.Copy, scale=-1.0).then_inc(neg3, 1)
            squares(14, 2, 7)
            roots(14, 2)
            squares(15, 3, 7)
            measured_squares(0, 0)
            norm_squares(6, 0)
            roots(15, 3)
            norm_root(6, 0)
            measured_squares(0, 1)
            evac_sup(6)
            amplitude(0, 0)
            measured_squares(0, 2)
            amplitude(0, 1)
            measured_squares(0, 3)
            amplitude(0, 2)
            amplitude(0, 3)
            norm_squares(7, 2)
            norm_root(7, 2)
            evac_sup(7)
            row_root(0)
            row_root(1)
            measured_squares(1, 0)
            row_root(2)
            row_root(3)
            row_gelu(0)
            row_gelu(1)
            measured_squares(1, 1)
            amplitude(1, 0)
            row_gelu(2)
            row_gelu(3)
            amplitude(1, 1)
            measured_squares(1, 2)
            amplitude(1, 2)
            relu_1(0)
            measured_squares(1, 3)
            amplitude(1, 3)
            relu_2(0)
            result(0)
            for t in range(BT, T):
                row_root(t)
            for t in range(BT, T):
                row_gelu(t)
            relu_1(1)
            relu_2(1)
            result(1)

        @block.gpsimd
        def _(pool):
            def low(pos, slot, lo, hi):
                pool.wait_ge(hi_done, pos + 1)
                pool.tensor_tensor(lo, raw[slot][:, :].rearrange("p (k b) -> p k b", k=2) if len(lo.shape) == 3 else raw[slot][:, :],
                                   hi.bitcast(F32), ALU.subtract).then_inc(split_done, 1)

            def low_x(pos, slot, u):
                low(pos, slot, x_lo[:, 2 * u:2 * u + 2, :], x_hi[:, 2 * u:2 * u + 2, :])

            for u in range(U_X):
                low_x(u, u % RAW, u)
            with pool.Fori(0, HALVES) as half:
                for e in range(2):
                    fixed = X_FROM
                    with pool.Fori(0, fixed // RAW) as g:
                        for s in range(RAW):
                            low(stream_before(half, e) + g * RAW + s, s, w_lo[s % SPLIT][:, :], w_hi[s % SPLIT][:, :])
                    for u in range(fixed, fixed + 8):
                        pos = stream_pos(half, e, u)
                        k = (U_X + e * U_PASS + u + (u - fixed if e else 0)) % RAW
                        low(pos, k, w_lo[u % SPLIT][:, :], w_hi[u % SPLIT][:, :])
                        if e:
                            low_x(pos + 1, (k + 1) % RAW, u - fixed)
                    with pool.Fori(fixed // RAW + 2, U_PASS // RAW) as g:
                        for s in range(RAW):
                            low(stream_before(half, e) + (U_X if e else 0) + g * RAW + s, s,
                                w_lo[s % SPLIT][:, :], w_hi[s % SPLIT][:, :])

            def low_s(t, slot):
                for e in range(2):
                    for kd in range(KD):
                        u = e * 2 + kd // 2
                        pool.wait_ge(s_high, t * 8 + e * 4 + kd + 1)
                        src = raw[u][:, kd % 2 * 512:kd % 2 * 512 + 512].rearrange("p (n s b) -> p s n b", n=N, s=SUB)
                        low = pool.tensor_tensor(s_lo[slot][:, e, kd, :].rearrange("p (s n b) -> p s n b", n=N, s=SUB), src,
                                                 s_hi[slot][:, e, kd, :].bitcast(F32).rearrange("p (s n b) -> p s n b", n=N, s=SUB),
                                                 ALU.subtract)
                        if kd % 2:
                            low.then_inc(split_done, 1)

            low_s(0, 0)
            with pool.Fori(0, 3) as i:
                low_s(2 * i + 1, 1)
                low_s(2 * i + 2, 0)
            low_s(7, 1)
            low_s(8, 0)
            for u in range(U_X):
                low_x(U_A + u, u % RAW, u)

            def wide(q, t, sub):
                pool.wait_ge(av_mm, q + 1)
                for z, u, done in ((0, u_hi[:, :, :, :].bitcast(F32), wt_high), (1, u_lo[:, :, :, :], wt_done)):
                    src = u[:, t, sub, :] if isinstance(t, int) else u[:, bass.ds(t, 1), sub, :].rearrange("p o x -> p (o x)")
                    pool.tensor_tensor(wt[sub % 2][:, z, :, :].rearrange("p h (n b) -> p (h n) b", n=N),
                                       src.unsqueeze(2).to_broadcast((P, H * N, 32)),
                                       mask[:, :].unsqueeze(1).to_broadcast((P, H * N, 32)), ALU.mult).then_inc(done, 1)

            def low_sv(t):
                for e in range(2):
                    for kd in range(KD):
                        u = e * 2 + kd // 2
                        pool.wait_ge(s_high, t * 8 + 8 * T + e * 4 + kd + 1)
                        src = raw[u][:, kd % 2 * 512:kd % 2 * 512 + 512].rearrange("p (n s b) -> p s n b", n=N, s=SUB)
                        low = pool.tensor_tensor(s_lo[0][:, e, kd, :].rearrange("p (s n b) -> p s n b", n=N, s=SUB), src,
                                                 s_hi[0][:, e, kd, :].bitcast(F32).rearrange("p (s n b) -> p s n b", n=N, s=SUB),
                                                 ALU.subtract)
                        if kd % 2:
                            low.then_inc(split_done, 1)

            pool.wait_ge(u_moved, 18)
            for sub in range(SUB):
                wide(sub, 0, sub)
            with pool.Fori(1, T) as t:
                low_sv(t)
                for sub in range(SUB):
                    wide(t * 4 + sub, t, sub)

            pool.wait_ge(ids_in, 16)
            for t in range(T):
                for i in range(N):
                    pool.indirect_dma_start(out=strength[:, t, i * N:i * N + N], out_offset=None, in_=tbls[i],
                                            in_offset=bass.IndirectOffsetOnAxis(ap=ids_t[:, t * N + i:t * N + i + 1], axis=0)
                                            ).then_inc(emb_in, 16)

            def half(f):
                return slice(f % 2 * W_COLS, f % 2 * W_COLS + W_COLS)

            def phasors(f, q):
                pool.wait_ge(rc_done, f + 1)
                z = z_t[q // 2 % 2][:, :, :, half(q)]
                for e in range(2):
                    last = pool.tensor_tensor(prod[q % 2][:, :, e, :], z[:, :, e, :], mag2[q % 2][:, :, :], ALU.mult)
                last.then_inc(u_done, 1)

            def weighted(f, q):
                pool.wait_ge(g_step, f * 12 + 12)
                z = z_t[q // 2 % 2][:, :, :, half(q)]
                for e in range(2):
                    last = pool.tensor_tensor(prod[q % 2][:, :, e, :], z[:, :, e, :], gsum[:, :, :], ALU.mult)
                last.then_inc(zg_done, 1)

            def cosines(f, q):
                pool.wait_ge(a_step, f * 16 + 16)
                flat = "p n e d -> p (n e d)"
                pool.tensor_tensor(acc[:, :, :, :].rearrange(flat), acc[:, :, :, :].rearrange(flat),
                                   prod[q % 2][:, :, :, :].rearrange(flat), ALU.mult).then_inc(ua_done, 1)
                pool.wait_ge(ua_done, f + 1)
                if not (isinstance(f, int) and f == 0):
                    pool.wait_ge(zg_done, f)
                pool.tensor_tensor(gsum[:, :, :], acc[:, :, 0, :], acc[:, :, 1, :], ALU.add).then_inc(g_done, 1)

            def sup_tile(t, par, first=False):
                for z in range(2):
                    f, q = 2 * t + z, 2 * par + z
                    phasors(f, q)
                    if not (first and z == 0):
                        weighted(f - 1, (q - 1) % 4)
                    cosines(f, q)

            sup_tile(0, 0, first=True)
            sup_tile(1, 1)
            with pool.Fori(1, T // 2 - 1) as i:
                sup_tile(2 * i, 0)
                sup_tile(2 * i + 1, 1)
            sup_tile(T - 2, 0)
            sup_tile(T - 1, 1)
            weighted(STEPS - 1, 3)
            for hf in range(HALVES):
                pool.wait_ge(fin_in[f"part{hf}"], 32)
                pool.tensor_tensor(part[hf][:, :, 0, :], part[hf][:, :, 0, :], part[hf][:, :, 1, :], ALU.add).then_inc(part_sum, 1)

        @block.vector
        def _(dve):
            def split_hidden(dve, it, k):
                dve.wait_ge(gelu_done, it(KH) + k + 1)
                dve.tensor_copy(hT_hi[:, k, :], gel[k % 2][:, :]).then_inc(hT_high, 1)
                dve.wait_ge(hT_high, it(KH) + k + 1)
                dve.tensor_tensor(hT_lo[:, k, :], gel[k % 2][:, :], hT_hi[:, k, :].bitcast(F32), ALU.subtract).then_inc(hT_done, 1)

            dve.sem_inc(h_evac, CREDIT_H)
            dve.sem_inc(s_evac, 1)
            dve.wait_ge(consts_in, 32)
            with dve.Fori(0, HALVES) as half:
                for e in range(2):
                    def it(n):
                        return half * (2 * n) + e * n

                    for hc in range(HC):
                        dve.wait_ge(w_used, it(U_PASS) + CREDIT_W + 8 * hc + 8)
                        dve.wait_ge(b1_in[hc % 2], it(HC // 2 * 16) + (hc // 2 + 1) * 16)
                        for bt in range(BT):
                            dve.tensor_tensor(h[:, bt, hc * 512:hc * 512 + 512], ps[:, (hc % 2) * 4 + bt, :],
                                              b1row[hc % 2][:, :], ALU.add).then_inc(h_evac, 1)
                        for bt in range(BT):
                            dve.wait_ge(h_evac, it(4 * HC) + CREDIT_H + 4 * hc + bt + 1)
                            dve.bn_stats(stats[:, bt, hc, :], h[:, bt, hc * 512:hc * 512 + 512]).then_inc(bn_done, 1)
                    dve.wait_ge(bn_done, it(BT * HC) + BT * HC)
                    dve.memset(std[:, 0, :], EPS).then_inc(norm_step, 1)
                    for bt in range(BT):
                        dve.bn_aggr(meanvar[:, bt, :], stats[:, bt, :, :].rearrange("p c s -> p (c s)")).then_inc(norm_step, 1)
                    dve.wait_ge(norm_step, it(BT + 2) + BT + 1)
                    dve.tensor_tensor(std[:, 0, :], meanvar[:, :, 1], std[:, 0, :], ALU.add).then_inc(var_done, 1)
                    dve.wait_ge(std_done, it(1) + 1)
                    dve.reciprocal(std[:, 2, :], std[:, 1, :]).then_inc(norm_step, 1)
                    dve.wait_ge(norm_step, it(BT + 2) + BT + 2)
                    for bt in range(BT):
                        dve.tensor_scalar(h[:, bt, :], h[:, bt, :], meanvar[:, bt, 0:1], std[:, 2, bt:bt + 1],
                                          ALU.subtract, ALU.mult).then_inc(ln_done, 1)

                    dve.wait_ge(w_used, it(U_PASS) + CREDIT_W + U_ENC1 + U_TOP)
                    for c in range(4):
                        dve.wait_ge(st_out[c % 2], it(160) + (c // 2) * 16 + 16)
                        dve.tensor_copy(stage[c % 2][:, :], ps[:, c, :]).then_inc(top_evac, 1)

                        if c == 1 or c == 3:
                            for k in range(2 * c - 2, 2 * c + 2):
                                split_hidden(dve, it, k)
                    for k in range(8, KH):
                        split_hidden(dve, it, k)

                    for oc in range(OC):
                        dve.wait_ge(w_used, it(U_PASS) + CREDIT_W + U_ENC1 + U_TOP + 2 * oc + 2)
                        dve.wait_ge(st_out[oc % 2], it(160) + (oc // 2 + 3) * 16)
                        dve.tensor_scalar(stage[oc % 2][:, :], ps[:, oc % 4, :], col(e * C_ENC + C_B2 + oc), None,
                                          ALU.add).then_inc(s_evac, 1)

            dve.sem_inc(qk_low, 4)
            dve.sem_inc(sc_masked, 4)
            for i in range(2):
                dve.wait_ge(st_out[i], ST_A)
            dve.wait_ge(mask_in, 16)

            def low_qk(g, c, slot):
                for a, m in enumerate(ORDER):
                    dve.wait_ge(qk_high, 4 * g + a + 1)
                    r = int(m == Q_I) if m in (Q_R, Q_I) else int(m == K_R)
                    x = q_t[slot] if m in (Q_R, Q_I) else k_t[slot]
                    dve.scalar_tensor_tensor(out=x[:, 1, r, :], in0=ps[:, a, :], scalar=col(C_QKVO + m * KD + c),
                                             in1=x[:, 0, r, :].bitcast(F32), op0=ALU.add, op1=ALU.subtract).then_inc(qk_low, 1)

            def own_scores(g, c, slot):
                if not (isinstance(g, int) and g == 0):
                    dve.wait_ge(sc_sum, g)
                for b in range(4):
                    dve.wait_ge(sc_mm, 8 + 4 * g + b + 1)
                    dve.tensor_tensor(masked[:, b, :].rearrange("p (g r) -> p g r", r=32),
                                      ps[:, 4 + b, :].rearrange("p (g r) -> p g r", r=32),
                                      mask[:, :].unsqueeze(1).to_broadcast((P, 16, 32)), ALU.mult).then_inc(sc_masked, 1)
                dve.wait_ge(sc_masked, 4 + 4 * g + 4)
                dve.tensor_reduce(score[slot][:, c * 8:c * 8 + 8, :, :].rearrange("p i a m -> p (i a m)"),
                                  masked[:, :, :].rearrange("p b (g r) -> p (b g) r", r=32), AX.X, ALU.add).then_inc(sc_sum, 1)

            def softmax_a(t, slot):
                base = t * SOFT_STEPS
                dve.wait_ge(sc_sum, t * 4 + 4)
                dve.tensor_tensor(square[:, :, :, :], score[slot][:, :, :, :], score[slot][:, :, :, :], ALU.mult).then_inc(soft, 1)
                dve.wait_ge(soft, base + 1)
                dve.scalar_tensor_tensor(out=square[:, :, 0, :], in0=square[:, :, 0, :], scalar=1e-8,
                                         in1=square[:, :, 1, :], op0=ALU.add, op1=ALU.add).then_inc(soft, 1)

            def softmax_b(t):
                base = t * SOFT_STEPS
                dve.wait_ge(mag_done, t + 1)
                dve.tensor_reduce(red[:, 0, :], mag[:, :, :], AX.X, ALU.max).then_inc(soft, 1)
                dve.wait_ge(soft, base + 3)
                dve.tensor_tensor(mag[:, :, :], mag[:, :, :], red[:, 0, :].unsqueeze(2).to_broadcast((P, H * SUB, N)),
                                  ALU.subtract).then_inc(soft, 1)

            def softmax_c(t):
                base = t * SOFT_STEPS
                dve.wait_ge(exp_done, t + 1)
                dve.tensor_reduce(red[:, 1, :], mag[:, :, :], AX.X, ALU.add).then_inc(soft, 1)
                dve.wait_ge(soft, base + 5)
                dve.reciprocal(red[:, 2, :], red[:, 1, :]).then_inc(soft, 1)
                dve.wait_ge(soft, base + 6)
                dst = probs[:, t, :, :] if isinstance(t, int) else probs[:, bass.ds(t, 1), :, :].rearrange("p o i m -> p (o i) m")
                dve.tensor_tensor(dst, mag[:, :, :], red[:, 2, :].unsqueeze(2).to_broadcast((P, H * SUB, N)),
                                  ALU.mult).then_inc(soft, 1)

            def score_tile(t, par, first=False):
                for c in range(KD):
                    low_qk(t * 4 + c, c, c % 2)
                    if not (first and c == 0):
                        own_scores(t * 4 + c - 1, (c - 1) % 4, par if c else 1 - par)
                    if not first:
                        if c == 0:
                            softmax_a(t - 1, 1 - par)
                        if c == 1:
                            softmax_b(t - 1)
                        if c == 2:
                            softmax_c(t - 1)

            score_tile(0, 0, first=True)
            with dve.Fori(0, 3) as i:
                score_tile(2 * i + 1, 1)
                score_tile(2 * i + 2, 0)
            score_tile(7, 1)
            own_scores(CH - 1, 3, 1)
            dve.wait_ge(bv_high, 2)
            for z in range(2):
                dve.tensor_tensor(bv_lo[:, :, z], col(C_QKVO + V_R * KD, 2 * KD), bv_hi[:, :, z].bitcast(F32),
                                  ALU.subtract).then_inc(bv_low, 1)
            softmax_a(7, 1)
            softmax_b(7)
            softmax_c(7)

            dve.wait_ge(soft, T * SOFT_STEPS)
            for n in range(N):
                for m in range(N):
                    dve.tensor_copy(u_lo[32 * m:32 * m + 32, :, :, :].rearrange("p t s (h n) -> p t s h n", n=N)[:, :, :, :, n],
                                    probs[32 * n:32 * n + 32, :, :, m].rearrange("p t (h s) -> p t s h", s=SUB)).then_inc(u_moved, 1)
            dve.wait_ge(u_moved, 16)
            dve.tensor_copy(u_hi[:, :, :, :], u_lo[:, :, :, :]).then_inc(u_moved, 1)
            dve.wait_ge(u_moved, 17)
            dve.tensor_tensor(u_lo[:, :, :, :], u_lo[:, :, :, :], u_hi[:, :, :, :].bitcast(F32), ALU.subtract).then_inc(u_moved, 1)

            def low_v(q, sub):
                for e in range(2):
                    dve.wait_ge(v_high, 2 * q + e + 1)
                    dve.tensor_tensor(v_t[sub % 2][:, 1, :, e, :], ps[:, sub % 2 * 2 + e, :].rearrange("p (h d) -> p h d", h=H),
                                      v_t[sub % 2][:, 0, :, e, :].bitcast(F32), ALU.subtract).then_inc(v_low, 1)

            def low_o(q, sub):
                b = 4 + sub % 2 * 2
                for e in range(2):
                    for hh in range(2):
                        rows = slice(HD * hh, HD * hh + HD)
                        dve.wait_ge(o_high, 4 * q + 2 * e + 2)
                        dve.tensor_tensor(o_lo[rows, e, :, sub * P:sub * P + P],
                                          ps[HD * e:HD * e + HD, b:b + 2, :].rearrange("p k (c z q) -> p (k c) z q", c=2, z=2)[:, :, hh, :],
                                          o_hi[rows, e, :, sub * P:sub * P + P].bitcast(F32), ALU.subtract).then_inc(o_low, 1)

            def value_tile(t, first=False):
                for sub in range(SUB):
                    low_v(t * 4 + sub, sub)
                    if sub:
                        low_o(t * 4 + sub - 1, sub - 1)
                low_o(t * 4 + 3, 3)

            value_tile(0)
            dve.wait_ge(bias_mm, 1)
            dve.tensor_tensor(bo_t[:, :], ps[:, 4, 0:16].rearrange("p (j z) -> p j z", z=2)[:, :, 0],
                              col(C_QKVO + O_R * KD, 2 * KD), ALU.add).then_inc(bias_done, 1)
            with dve.Fori(1, T) as t:
                value_tile(t)

            def magnitudes(f, q):
                s = q % 2
                dve.wait_ge(sq_done, f + 1)
                dve.tensor_tensor(mag2[s][:, :, :], prod[s][:, :, 0, :], prod[s][:, :, 1, :], ALU.add).then_inc(m_step, 1)
                dve.wait_ge(m_step, f * 3 + 1)
                dve.tensor_scalar(zero[s][:, :, :], mag2[s][:, :, :], 0.0, None, ALU.is_equal).then_inc(m_step, 1)
                dve.wait_ge(m_step, f * 3 + 2)
                dve.tensor_tensor(mag2[s][:, :, :], mag2[s][:, :, :], zero[s][:, :, :], ALU.add).then_inc(m_step, 1)

            def reciprocals(f, q):
                s = q % 2
                dve.wait_ge(rt_done, f + 1)
                dve.reciprocal(mag2[s][:, :, :], mag2[s][:, :, :]).then_inc(rc_done, 1)

            def strengths(t, par):
                dve.wait_ge(emb_in, 16 * N * T)
                if not (isinstance(t, int) and t < 2):
                    dve.wait_ge(g_step, t * 24 - 24)
                src = strength[:, bass.ds(t, 1), :].rearrange("p o x -> p (o x)")
                dve.tensor_copy(st_cur[par][:, :], src).then_inc(cur, 1)

            def sums(f, q):
                par, s = q // 2 % 2, q % 2
                dve.wait_ge(u_done, f + 1)
                if not (isinstance(f, int) and f == 0):
                    dve.wait_ge(g_done, f)
                dve.wait_ge(cur, (f - s) // 2 + 1 if isinstance(f, int) else tile_of[0] + 1)
                for i in range(N):
                    for j in range(N):
                        st = st_cur[par][:, i * N + j:i * N + j + 1]
                        u = prod[s][:, i, :, :].rearrange("p e d -> p (e d)")
                        a = acc[:, j, :, :].rearrange("p e d -> p (e d)")
                        if i == 0:
                            dve.tensor_scalar(a, u, st, None, ALU.mult).then_inc(a_step, 1)
                        else:
                            dve.wait_ge(a_step, f * 16 + 4 * (i - 1) + j + 1)
                            dve.scalar_tensor_tensor(out=a, in0=u, scalar=st, in1=a, op0=ALU.mult, op1=ALU.add).then_inc(a_step, 1)

            def vanished(f, q):
                par, s = q // 2 % 2, q % 2
                dve.wait_ge(g_done, f + 1)
                for d in range(1, N):
                    for j in range(N):
                        i = (j + d) % N
                        if d > 1:
                            dve.wait_ge(g_step, f * 12 + 4 * (d - 2) + j + 1)
                        dve.scalar_tensor_tensor(out=gsum[:, j, :], in0=zero[s][:, i, :], scalar=st_cur[par][:, i * N + j:i * N + j + 1],
                                                 in1=gsum[:, j, :], op0=ALU.mult, op1=ALU.add).then_inc(g_step, 1)

            def total(f, q):
                par, s = q // 2 % 2, q % 2
                cols_ = slice(s * W_COLS, s * W_COLS + W_COLS)
                dve.wait_ge(zg_done, f + 1)
                flat = "p n e d -> p (n e d)"
                dve.tensor_tensor(prod[s][:, 0:2, :, :].rearrange(flat), prod[s][:, 0:2, :, :].rearrange(flat),
                                  prod[s][:, 2:4, :, :].rearrange(flat), ALU.add).then_inc(t_step, 1)
                dve.wait_ge(t_step, f * 2 + 1)
                if not (isinstance(f, int) and f < 4):
                    dve.wait_ge(st_mm, tile_of[1] * 2 - 2)
                dve.tensor_tensor(sup_t[par][:, :, cols_], prod[s][:, 0, :, :], prod[s][:, 1, :, :], ALU.add).then_inc(t_step, 1)

            def norm_eps(t, par):
                dve.wait_ge(nrm_sq, t + 1)
                dve.tensor_scalar(norm[:, 1, par:par + 1], norm[:, 0, par:par + 1], 1e-8, None, ALU.add).then_inc(nrm_a, 1)

            def norm_rows(t, par):
                dve.wait_ge(nrm_rt, t + 1)
                dve.reciprocal(norm[:, 3, par:par + 1], norm[:, 2, par:par + 1]).then_inc(nrm_b, 1)
                dve.wait_ge(nrm_b, t * 2 + 1)
                dve.tensor_scalar(sup_t[par][:, :, :], sup_t[par][:, :, :], norm[:, 3, par:par + 1], None, ALU.mult).then_inc(nrm_b, 1)

            tile_of = [0, 0]

            def amplitude_sum(hf, c):
                dve.wait_ge(me_sq, (hf * KD + c + 1) * 2)
                dve.tensor_tensor(amp_T[:, hf, c, :], sq[:, c % 2 * 2, :], sq[:, c % 2 * 2 + 1, :], ALU.add).then_inc(me_sum, 1)

            def row_stats(t):
                dve.wait_ge(row_mm, t + 1)
                if t == 0:
                    dve.wait_ge(fin_in["postb"], 16)
                if t >= BT:
                    dve.wait_ge(row_tr, t - BT + 1)
                dve.tensor_tensor(row_t[t % BT], ps[:, 4 + t % 2, :], postb[:, :], ALU.add).then_inc(row_in, 1)
                dve.wait_ge(row_in, t + 1)
                dve.bn_stats(stats2[:, t, :], row_t[t % BT]).then_inc(row_bn, 1)
                dve.wait_ge(row_bn, t + 1)
                dve.bn_aggr(mv2[:, t, :], stats2[:, t, :]).then_inc(row_mv, 1)
                dve.wait_ge(row_mv, t + 1)
                dve.tensor_scalar(std2[:, 0, t:t + 1], mv2[:, t, 1:2], EPS, None, ALU.add).then_inc(row_var, 1)

            def row_norm(t):
                dve.wait_ge(row_std, t + 1)
                dve.reciprocal(std2[:, 2, t:t + 1], std2[:, 1, t:t + 1]).then_inc(row_rstd, 1)
                dve.wait_ge(row_rstd, t + 1)
                dve.tensor_scalar(row_t[t % BT], row_t[t % BT], mv2[:, t, 0:1], std2[:, 2, t:t + 1],
                                  ALU.subtract, ALU.mult).then_inc(row_ln, 1)

            def top_sum(hf):
                dve.wait_ge(part_sum, hf + 1)
                for c in range(KD):
                    dve.wait_ge(t1_mm, hf * KD + c + 1)
                    dve.tensor_tensor(h1_T[:, c, :], ps[:, 4 + c, :], part[hf][:, c, 0, :], ALU.add).then_inc(t1_sum, 1)

            def sup_tile(t, par, first=False, last=False):
                strengths(t, par)
                for z in range(2):
                    f, q = 2 * t + z, 2 * par + z
                    reciprocals(f, q)
                    if not (first and z == 0):
                        vanished(f - 1, (q - 1) % 4)
                    tile_of[0] = t
                    sums(f, q)
                    if last and z:
                        amplitude_sum(0, 0)
                    if not (first and z == 0):
                        tile_of[1] = t if z else t - 1
                        total(f - 1, (q - 1) % 4)
                    if not (last and z):
                        magnitudes(f + 1, (q + 1) % 4)
                    if z == 0 and not first:
                        norm_eps(t - 1, 1 - par)
                        norm_rows(t - 1, 1 - par)

            magnitudes(0, 0)
            sup_tile(0, 0, first=True)
            sup_tile(1, 1)
            with dve.Fori(1, T // 2 - 1) as i:
                sup_tile(2 * i, 0)
                sup_tile(2 * i + 1, 1)
            sup_tile(T - 2, 0)
            sup_tile(T - 1, 1, last=True)
            amplitude_sum(0, 1)
            vanished(STEPS - 1, 3)
            amplitude_sum(0, 2)
            amplitude_sum(0, 3)
            tile_of[1] = T - 1
            total(STEPS - 1, 3)
            norm_eps(T - 1, 1)
            norm_rows(T - 1, 1)
            row_stats(0)
            row_stats(1)
            row_norm(0)
            row_norm(1)
            row_stats(2)
            row_stats(3)
            row_norm(2)
            row_norm(3)
            amplitude_sum(1, 0)
            amplitude_sum(1, 1)
            amplitude_sum(1, 2)
            top_sum(0)
            amplitude_sum(1, 3)
            row_stats(4)
            row_stats(5)
            row_norm(4)
            row_norm(5)
            row_stats(6)
            row_stats(7)
            row_norm(6)
            row_norm(7)
            top_sum(1)

        @block.tensor
        def _(pe):
            pe.sem_inc(w_used, CREDIT_W)
            pe.wait_ge(consts_in, 32)
            with pe.Fori(0, HALVES) as half:
                for e in range(2):
                    def it(n):
                        return half * (2 * n) + e * n

                    def unit(u, s):
                        pe.wait_ge(split_done, stream_pos(half, e, u, not isinstance(u, int) and late[0]) + 1)
                        return w_hi[s], w_lo[s]

                    late = [False]
                    with pe.Fori(0, HC // 2) as hp:
                        for par in range(2):
                            if par == 0:
                                pe.wait_ge(s_evac, it(OC) + 1)
                            pe.wait_ge(h_evac, it(4 * HC) + hp * 8 + par * 4 + 4)
                            for j in range(8):
                                wh, wl = unit(hp * 16 + par * 8 + j, j % 2)
                                for kk in range(2):
                                    k = 2 * j + kk
                                    for bt in range(BT):
                                        b = slice(bt * P, bt * P + P)
                                        w = slice(kk * 512, kk * 512 + 512)
                                        last = mm3(pe, ps[:, par * 4 + bt, :], x_hi[:, k, b], x_lo[:, k, b],
                                                   wh[:, w], wl[:, w], k == 0, k == KX - 1)
                                last.then_inc(w_used, 1)
                    pe.wait_ge(h_evac, it(4 * HC) + CREDIT_H + 12)
                    for j in range(U_TOP):
                        wh, wl = unit(U_ENC1 + j, j % 2)
                        for kk in range(2):
                            k = e * 8 + 2 * j + kk
                            for c in range(4):
                                w = slice(kk * 512 + c * P, kk * 512 + c * P + P)
                                last = mm3(pe, ps[:, c, :], wh[:, w], wl[:, w], x_hi[:, k, :], x_lo[:, k, :],
                                           2 * j + kk == 0, 2 * j + kk == 7)
                        last.then_inc(w_used, 1)

                    def turn(k):
                        if k >= 4:
                            pe.wait_ge(gelu_done, it(KH) + k - 3)
                        for bt in range(BT):
                            last = pe.transpose(ps[:, 4 + k % 4, bt * P:bt * P + P], h[:, bt, k * P:k * P + P], ident[:, :])
                        last.then_inc(tr_done, 1)

                    pe.wait_ge(ln_done, it(BT) + BT)
                    for k in range(4):
                        turn(k)

                    def second(oc, q, first=False):
                        for v in range(2):
                            wh, wl = unit(U_ENC1 + U_TOP + 2 * oc + v, v)
                            for kk in range(8):
                                k = v * 8 + kk
                                if first:
                                    pe.wait_ge(hT_done, it(KH) + k + 1)
                                w = slice(kk * P, kk * P + P)
                                last = mm3(pe, ps[:, q, :], wh[:, w], wl[:, w], hT_hi[:, k, :], hT_lo[:, k, :],
                                           k == 0, k == KH - 1)
                                if kk == 7:
                                    last.then_inc(w_used, 1)
                                if first and k + 4 < KH:
                                    turn(k + 4)

                    for oc in range(8):
                        if oc < 4:
                            pe.wait_ge(top_evac, it(4) + oc + 1)
                        else:
                            pe.wait_ge(s_evac, it(OC) + oc - 2)
                        second(oc, oc % 4, oc == 0)
                    late = [True]
                    with pe.Fori(2, OC // 4) as og:
                        for q in range(4):
                            pe.wait_ge(s_evac, it(OC) + og * 4 + q - 2)
                            second(og * 4 + q, q)

            pe.sem_inc(sc_mm, 8)

            def project(g, t, c, par):
                for a, m in enumerate(ORDER):
                    pe.wait_ge(qk_low, 4 * g + a + 1)
                    if isinstance(g, int) and g == 0:
                        pe.wait_ge(s_evac, 1 + 4 * OC)
                    e = m % 2
                    for kd in range(KD):
                        if c == 0 and kd % 2 == 0:
                            pe.wait_ge(split_done, 4 * t + U_A + 2 * e + kd // 2 + 1)
                        w = slice(c * P, c * P + P)
                        last = mm3(pe, ps[:, a, :], x_hi[:, 4 * m + kd, w], x_lo[:, 4 * m + kd, w],
                                   s_hi[par][:, e, kd, :], s_lo[par][:, e, kd, :], kd == 0, kd == KD - 1)
                    last.then_inc(qk_mm, 1)

            def scores(g, slot):
                pe.wait_ge(qk_low, 4 + 4 * g + 4)
                pe.wait_ge(neg_done, g + 1)
                for hh in range(2):
                    rows = slice(HD * hh, HD * hh + HD)
                    for sub in range(SUB):
                        idx = hh * SUB + sub
                        out = ps[:, 4 + idx // 2, (idx % 2) * 256:(idx % 2) * 256 + 256]
                        if idx % 2 == 0:
                            pe.wait_ge(sc_masked, 4 * g + idx // 2 + 1)
                        for r, k0 in ((0, 1), (1, 0)):
                            q = [q_t[slot][rows, z, r, :][:, sub * P:sub * P + P] for z in range(2)]
                            k = [k_t[slot][rows, z, k0:k0 + 2, sub * P:sub * P + P]
                                 for z in range(2)]
                            last = mm3(pe, out, q[0], q[1], k[0], k[1], r == 0, r == 1)
                        if idx % 2 == 1:
                            last.then_inc(sc_mm, 1)

            def score_tile(t, par, first=False):
                for c in range(KD):
                    project(t * 4 + c, t, c, par)
                    if not (first and c == 0):
                        scores(t * 4 + c - 1, (c - 1) % 2)

            score_tile(0, 0, first=True)
            with pe.Fori(0, 3) as i:
                score_tile(2 * i + 1, 1)
                score_tile(2 * i + 2, 0)
            score_tile(7, 1)
            scores(CH - 1, 1)

            pe.sem_inc(av_mm, 2)

            def values(t, sub):
                first = isinstance(t, int)
                q = t * 4 + sub
                for e in range(2):
                    b = sub % 2 * 2 + e
                    if sub >= 2:
                        pe.wait_ge(v_low, 2 * q + e - 3)
                    elif first:
                        pe.wait_ge(qk_low, 4 + 4 * CH)
                    else:
                        pe.wait_ge(wo_evac, t * 8 + b - 3)
                    for kd in range(KD):
                        if sub == 0 and kd % 2 == 0:
                            if first:
                                pe.wait_ge(split_done, U_B + RAW + 2 * e + kd // 2 + 1)
                            else:
                                pe.wait_ge(split_done, t * RAW + U_B + U_X + 2 * e + kd // 2 + 1)
                        x = slice(sub * P, sub * P + P)
                        last = mm3(pe, ps[:, b, :], s_hi[0][:, e, kd, x], s_lo[0][:, e, kd, x],
                                   x_hi[:, 4 * e + kd, :], x_lo[:, 4 * e + kd, :], kd == 0, kd == KD - 1)
                    last.then_inc(v_mm, 1)

            def attend(t, sub):
                first = isinstance(t, int)
                q = t * 4 + sub
                if first and sub < 2:
                    pe.wait_ge(sc_masked, 4 + 4 * CH)
                else:
                    pe.wait_ge(o_low, 4 * q - 4)
                if not first and sub == 0:
                    pe.wait_ge(bias_done, 1)
                pe.wait_ge(v_low, 2 * q + 2)
                pe.wait_ge(wt_done, q + 1)
                for hd in range(H):
                    v = [v_t[sub % 2][:, z, hd, :, :].rearrange("p e d -> p (e d)") for z in range(2)]
                    w = [wt[sub % 2][:, z, hd, :] for z in range(2)]
                    last = mm3(pe, ps[:, 4 + sub % 2 * 2 + hd // 4, hd % 4 * P:hd % 4 * P + P], v[0], v[1], w[0], w[1], True, True)
                last.then_inc(av_mm, 1)

            def outputs(t):
                for j in range(8):
                    e, c = j // 4, j % 4
                    if c == 0:
                        pe.wait_ge(o_low, t * 16 + 14 + 2 * e)
                    if j >= 4:
                        pe.wait_ge(wo_evac, t * 8 + j - 3)
                    w = slice(c * P, c * P + P)
                    for kd in range(KD):
                        k = 8 + 4 * e + kd
                        last = mm3(pe, ps[:, c, :], x_hi[:, k, w], x_lo[:, k, w], o_hi[:, e, kd, :], o_lo[:, e, kd, :],
                                   kd == 0, kd == KD - 1)
                    last.then_inc(wo_mm, 1)

            def value_tile(t):
                values(t, 0)
                for sub in range(1, SUB):
                    values(t, sub)
                    attend(t, sub - 1)
                attend(t, 3)
                if isinstance(t, int):
                    pe.wait_ge(split_done, U_B + RAW + U_X)
                    pe.wait_ge(bv_low, 2)
                    pe.wait_ge(o_low, 12)
                    for j in range(8):
                        e, w = j // 4, slice(j % 4 * P, j % 4 * P + P)
                        for kd in range(KD):
                            k = 8 + 4 * e + kd
                            last = mm3(pe, ps[:, 4, 2 * j:2 * j + 2], x_hi[:, k, w], x_lo[:, k, w],
                                       bv_hi[:, 4 * e + kd, :], bv_lo[:, 4 * e + kd, :], kd == 0, kd == KD - 1)
                    last.then_inc(bias_mm, 1)
                outputs(t)

            value_tile(0)
            with pe.Fori(1, T) as t:
                value_tile(t)

            def interfere(t, n):
                first = isinstance(t, int) and t == 0
                w = (int_a, int_b)[n // 2][:, n % 2, :, :, :]
                a = at_t[n % 2]
                if first:
                    pe.wait_ge(int_in[n], 16)
                for e in range(2):
                    b = n % 2 * 2 + e
                    if first and n < 2:
                        pe.wait_ge(wo_evac, 8 * T)
                    else:
                        pe.wait_ge(z_evac, t * 8 + 2 * n + e - 3)
                    pe.wait_ge(neg2, t * 4 + n + 1)
                    for part in range(2):
                        src = part if e else 2 * part
                        for k in range(KD):
                            last = pe.matmul(ps[:, b, :], a[:, src, k, :], w[:, part ^ e, k, :],
                                             start=(part == 0 and k == 0), stop=(part == 1 and k == KD - 1))
                    last.then_inc(z_mm, 1)

            def turn_sup(t, par):
                pe.wait_ge(nrm_b, t * 2 + 2)
                if not (isinstance(t, int) and t == 0):
                    pe.wait_ge(st_evac, t * 2)
                elif t == 0:
                    pe.wait_ge(o_low, 16 * T)
                for e in range(2):
                    for k in range(KD):
                        last = pe.transpose(ps[:, 6 + e, k * P:k * P + P], sup_t[par][:, e, k * P:k * P + P], ident[:, :])
                    last.then_inc(st_mm, 1)

            def sup_tile(t, par):
                for n in range(N):
                    interfere(t, n)
                if not isinstance(t, int) or t >= 2:
                    turn_sup(t - 2, par)

            sup_tile(0, 0)
            sup_tile(1, 1)
            sup_tile(2, 0)
            sup_tile(3, 1)
            with pe.Fori(2, T // 2) as i:
                sup_tile(2 * i, 0)
                sup_tile(2 * i + 1, 1)

            def measure(hf, c):
                g = hf * KD + c
                if g == 0:
                    pe.wait_ge(neg3, 1)
                if g < 2:
                    pe.wait_ge(z_evac, 8 * T)
                else:
                    pe.wait_ge(me_sq, 2 * g - 2)
                pe.wait_ge(st_evac, (hf + 1) * T)
                for e in range(2):
                    for src in range(2):
                        w = meas_neg if src and not e else meas[:, src ^ e, :, :]
                        for k in range(KD):
                            last = pe.matmul(ps[:, c % 2 * 2 + e, :], w[:, k, c * P:c * P + P], sup_T[:, src, k, hf * HB:hf * HB + HB],
                                             start=(src == 0 and k == 0), stop=(src == 1 and k == KD - 1))
                last.then_inc(me_mm, 1)

            def post(t):
                hf, b = t // BT, 4 + t % 2
                pe.wait_ge(fin_in["post"], 16)
                pe.wait_ge(amp, (hf + 1) * KD)
                if t % BT >= 2:
                    pe.wait_ge(row_in, t - 1)
                elif hf:
                    pe.wait_ge(t2_relu, 2)
                for k in range(KD):
                    last = pe.matmul(ps[:, b, :], amp_T[:, hf, k, t % BT * P:t % BT * P + P], post_wt[:, k, :],
                                     start=(k == 0), stop=(k == KD - 1))
                last.then_inc(row_mm, 1)

            def turn_row(t):
                pe.wait_ge(row_ln, t + 1)
                if t < 2:
                    pe.wait_ge(st_evac, 2 * T)
                elif t % BT >= 2:
                    pe.wait_ge(z_gelu, (t - 1) * KD)
                else:
                    pe.wait_ge(y_done, 1)
                for k in range(KD):
                    last = pe.transpose(ps[:, 6 + t % 2, k * P:k * P + P], row_t[t % BT][:, k * P:k * P + P], ident[:, :])
                last.then_inc(row_tr, 1)

            def top_1(hf):
                pe.wait_ge(fin_in["topz"], 16)
                pe.wait_ge(z_gelu, (hf + 1) * BT * KD)
                for c in range(KD):
                    for k in range(KD):
                        last = pe.matmul(ps[:, 4 + c, :], topz[:, k, c * P:c * P + P], z_out[hf][:, k, :],
                                         start=(k == 0), stop=(k == KD - 1))
                    last.then_inc(t1_mm, 1)

            def top_2(hf):
                pe.wait_ge(fin_in["top2"], 16)
                pe.wait_ge(t1_relu, (hf + 1) * KD)
                for c in range(2):
                    for k in range(KD):
                        last = pe.matmul(ps[:, 4 + c, :], top2_wt[:, k, c * P:c * P + P], h1_T[:, k, :],
                                         start=(k == 0), stop=(k == KD - 1))
                    last.then_inc(t2_mm, 1)

            def top_3(hf):
                pe.wait_ge(t2_relu, (hf + 1) * 2)
                for k in range(2):
                    last = pe.matmul(ps[0:1, 6, :], col(C_W3 + k), h2_T[:, k, :], start=(k == 0), stop=(k == 1))
                last.then_inc(y_mm, 1)

            pe.wait_ge(fin_in["meas"], 16)
            measure(0, 0)
            measure(0, 1)
            turn_sup(T - 2, 0)
            measure(0, 2)
            measure(0, 3)
            post(0)
            post(1)
            turn_sup(T - 1, 1)
            measure(1, 0)
            post(2)
            post(3)
            turn_row(0)
            turn_row(1)
            measure(1, 1)
            turn_row(2)
            turn_row(3)
            measure(1, 2)
            top_1(0)
            measure(1, 3)
            top_2(0)
            top_3(0)
            for t in range(BT, T):
                post(t)
            for t in range(BT, T):
                turn_row(t)
            top_1(1)
            top_2(1)
            top_3(1)


def chunks(w):
    return w.reshape(-1, P, w.shape[1]).transpose(1, 0, 2).reshape(P, -1)


def pair(wr, wi):
    import numpy as np
    return np.concatenate([chunks(wr.T), chunks(wi.T)], 1)


def lay_out(i, np):
    x = i["r_x"]
    xu = np.empty((4, U_X, P, UNIT), x.dtype)
    for hf in range(2):
        xu[hf] = x[hf * HB:(hf + 1) * HB].T.reshape(U_X, 2, P, HB).transpose(0, 2, 1, 3).reshape(U_X, P, UNIT)
    for m, n in enumerate(("Wq_r", "Wq_i", "Wk_r", "Wk_i", "Wv_r", "Wv_i", "Wo_r", "Wo_i")):
        xu[2 + m // 4, 2 * (m % 4):2 * (m % 4) + 2] = i["L0_rec_" + n].T.reshape(2, 2, P, D).transpose(0, 2, 1, 3).reshape(2, P, UNIT)
    wu = np.empty((2, U_PASS, P, UNIT), x.dtype)
    top = i["W_top1"][D:].reshape(2, U_TOP, 2, P, 512).transpose(0, 1, 3, 2, 4).reshape(2, U_TOP, P, UNIT)
    for e, n in enumerate(("er", "ei")):
        w1, w2 = i[f"L0_rec_{n}_W1"], i[f"L0_rec_{n}_W2"]
        wu[e, :U_ENC1] = w1.T.reshape(KX // 2, 2, P, HC, 512).transpose(3, 0, 2, 1, 4).reshape(U_ENC1, P, UNIT)
        wu[e, U_ENC1:U_ENC1 + U_TOP] = top[e]
        wu[e, U_ENC1 + U_TOP:] = w2.T.reshape(2, 8, P, OC, P).transpose(3, 0, 2, 1, 4).reshape(U_ENC2, P, UNIT)
    b1 = np.stack([i["L0_rec_er_b1"], i["L0_rec_ei_b1"]])
    c = []
    for n in ("er", "ei"):
        for v in ("g1", "be1", "b2"):
            c.append(i[f"L0_rec_{n}_{v}"].reshape(-1, P).T)
    for n in ("bq_r", "bq_i", "bk_r", "bk_i", "bv_r", "bv_i", "bo_r", "bo_i"):
        c.append(i["L0_rec_" + n].reshape(-1, P).T)
    c += [i["b_top1"].reshape(-1, P).T, i["b_top2"].reshape(-1, P).T, i["W_top3"].reshape(-1, P).T]
    c += [i["L0_rec_post_g"].reshape(-1, P).T, i["L0_rec_post_be"].reshape(-1, P).T]
    cols = np.ascontiguousarray(np.concatenate(c, 1))
    eye = np.eye(P, dtype=np.float32)
    return {"x_units": xu, "w_units": wu, "b1": b1, "cols": cols, "eye": eye, "mask_d": np.tile(np.eye(32, dtype=np.float32), (4, 1)),
            "ids": np.ascontiguousarray(i["ids"].reshape(T, P, N).transpose(1, 0, 2).reshape(P, T * N)),
            "int_w": np.stack([pair(i["L0_rec_int_Wr"][n], i["L0_rec_int_Wi"][n]) for n in range(N)]),
            "meas_w": pair(i["L0_rec_meas_Mr"], i["L0_rec_meas_Mi"]),
            "post_w": chunks(i["L0_rec_post_W"].T), "post_b": i["L0_rec_post_b"].reshape(1, D),
            "topz_w": chunks(i["W_top1"][:D]), "top2_w": chunks(i["W_top2"])}


def kernel(**inputs):
    import numpy as np
    import concourse.bacc as bacc
    from concourse.bass_utils import run_bass_kernel_spmd

    nc = bacc.Bacc("TRN2", target_bir_lowering=False, num_devices=1)
    inputs = {k: np.asarray(v) for k, v in inputs.items()}
    laid = lay_out(inputs, np)
    arrays = {f"in_{name}": a for name, a in laid.items()}
    arrays.update({f"in_tbl_{n}": inputs[f"tbl_{n}"] for n in range(N)})
    aps = {name[3:]: nc.dram_tensor(name, a.shape, mybir.dt.from_np(a.dtype), kind="ExternalInput").ap() for name, a in arrays.items()}
    tbls = [aps.pop(f"tbl_{n}") for n in range(N)]
    s_T = nc.dram_tensor("s_T", (2, T, P, KD, N, P), F32).ap()
    top_part = nc.dram_tensor("top_part", (2, KD, P, B), F32).ap()
    at_T = nc.dram_tensor("at_T", (T, N, P, 2, KD, P), F32).ap()
    y = nc.dram_tensor("out_y", (1, B), F32, kind="ExternalOutput").ap()
    build(nc, **aps, tbls=tbls, s_T=s_T, top_part=top_part, at_T=at_T, y=y)
    r = run_bass_kernel_spmd(nc, [arrays], core_ids=[0])
    return r.results[0]["out_y"].reshape(B, 1)
```

```python
import concourse.bass as bass
from concourse import mybir
from contextlib import ExitStack

F32 = mybir.dt.float32
F32R = mybir.dt.float32r
I32 = mybir.dt.int32
ACT = mybir.ActivationFunctionType
ALU = mybir.AluOpType
AX = mybir.AxisListType

P = 128
B = 1024
HALVES = 2
HB = B // HALVES
BT = HB // P
IN = 2048
KX = IN // P
HID = 2048
HC = HID // 512
KH = HID // P
D = 512
KD = D // P
N = 4
H = 8
HD = D // H
OC = N * D // P
UNIT = 1024
EPS = 1e-5
TINY = 2.0 ** -126

U_ENC1 = HC * KX * 512 // UNIT
U_TOP = KX // 2 * 512 // UNIT
U_ENC2 = OC * KH * P // UNIT
U_PASS = U_ENC1 + U_TOP + U_ENC2
U_X = KX * HB // UNIT
X_FROM = U_ENC1 + U_TOP + 8
U_HALF = 2 * U_PASS + U_X
RAW = 4
SPLIT = 2
CREDIT_W = SPLIT
CREDIT_H = 2 * BT

C_G, C_BE, C_B2, C_ENC = 0, KH, 2 * KH, 3 * KH
C_QKVO = 2 * C_ENC
C_TOP1 = C_QKVO + 8 * KD
C_TOP2 = C_TOP1 + KD
C_W3 = C_TOP2 + 2
C_POST = C_W3 + 2
C_ALL = C_POST + 2 * KD

T = B // P
SUB = P // 32
CH = T * KD
Q_R, Q_I, K_R, K_I, V_R, V_I, O_R, O_I = range(8)
SOFT_STEPS = 7
ORDER = (Q_R, K_R, K_I, Q_I)
U_A = U_X + HALVES * U_HALF
U_B = U_A + RAW * T
STEPS = 2 * T
W_COLS = D // 2
ST_A = 16 + HALVES * 2 * (OC + 4) // 2 * 16


def build(nc, x_units, w_units, b1, cols, eye, mask_d, bv, ids, tbls, int_w, meas_w, post_w, post_b, topz_w, top2_w,
          s_T, top_part, at_T, y):
    with ExitStack() as ctx:
        def sb(name, shape, dt, where=ctx):
            return where.enter_context(nc.sbuf_tensor(name, shape, dt))

        def sem(name):
            return ctx.enter_context(nc.semaphore(name))

        ps = ctx.enter_context(nc.psum_tensor("ps", [P, 8, 512], F32))

        colt = sb("colt", [P, C_ALL], F32)
        ident = sb("ident", [P, P], F32)
        ids_t = sb("ids_t", [P, T * N], I32)
        strength = sb("strength", [P, T, N * N], F32)
        strm = ctx.enter_context(ExitStack())
        raw = [sb(f"raw{i}", [P, UNIT], F32, strm) for i in range(RAW)]
        x_hi = sb("x_hi", [P, KX, HB], F32R, strm)
        x_lo = sb("x_lo", [P, KX, HB], F32R, strm)

        enc = ctx.enter_context(ExitStack())
        h = sb("h", [P, BT, HID], F32, enc)
        x_raw = h[:, :, :].rearrange("p t d -> p (t d)").rearrange("p (k b) -> p k b", k=KX)
        hT_hi = sb("hT_hi", [P, KH, HB], F32R, enc)
        hT_lo = sb("hT_lo", [P, KH, HB], F32R, enc)
        w_hi = [sb(f"w_hi{i}", [P, UNIT], F32R, enc) for i in range(SPLIT)]
        w_lo = [sb(f"w_lo{i}", [P, UNIT], F32R, enc) for i in range(SPLIT)]
        gel = [sb(f"gel{i}", [P, HB], F32, enc) for i in range(2)]
        stage = [sb(f"stage{i}", [P, HB], F32, enc) for i in range(2)]
        b1row = [sb(f"b1row{i}", [P, 512], F32, enc) for i in range(2)]
        stats = sb("stats", [P, BT, HC, 6], F32, enc)
        meanvar = sb("meanvar", [P, BT, 2], F32, enc)
        std = sb("std", [P, 3, BT], F32, enc)

        enc.close()
        att = ctx.enter_context(ExitStack())
        s_hi = [sb("s_hi0", [P, 2, KD, 512], F32R, att)]
        s_lo = [sb("s_lo0", [P, 2, KD, 512], F32R, att)]
        probs = sb("probs", [P, T, H * SUB, N], F32, att)
        mask = sb("mask", [P, 32], F32, att)
        sco = ctx.enter_context(ExitStack())
        s_hi.append(sb("s_hi1", [P, 2, KD, 512], F32R, sco))
        s_lo.append(sb("s_lo1", [P, 2, KD, 512], F32R, sco))
        q_t = [sb(f"q_t{i}", [P, 2, 2, 512], F32R, sco) for i in range(2)]
        k_t = [sb(f"k_t{i}", [P, 2, 2, 2, 512], F32R, sco) for i in range(2)]
        masked = sb("masked", [P, 2, 512], F32, sco)
        score = [sb(f"score{i}", [P, H * SUB, 2, N], F32, sco) for i in range(2)]
        square = sb("square", [P, H * SUB, 2, N], F32, sco)
        mag = sb("mag", [P, H * SUB, N], F32, sco)
        red = sb("red", [P, 3, H * SUB], F32, sco)

        sco.close()
        val = ctx.enter_context(ExitStack())
        bv_row = sb("bv_row", [P, 2, D], F32, val)
        v_t = [sb(f"v_t{i}", [P, H, 2, HD], F32, val) for i in range(2)]
        o_hi = sb("o_hi", [P, 2, KD, 512], F32R, val)
        o_lo = sb("o_lo", [P, 2, KD, 512], F32R, val)
        wt = [sb(f"wt{i}", [P, H, P], F32, val) for i in range(2)]
        u_t = sb("u_t", [P, T, SUB, H * N], F32, val)
        out_st = [sb(f"out_st{i}", [P, 512], F32, val) for i in range(4)]

        val.close()
        att.close()
        strm.close()
        sup = ctx.enter_context(ExitStack())
        at_t = [sb(f"at_t{i}", [P, 3, KD, P], F32, sup) for i in range(2)]
        zero = [sb("zero0", [P, N, W_COLS], F32, sup)]
        z_t = [sb(f"z_t{i}", [P, N, 2, D], F32, sup) for i in range(2)]
        sup_T = sb("sup_T", [P, 2, KD, B], F32, sup)
        int_a = sb("int_a", [P, 2, 2, KD, D], F32, sup)
        st_cur = [sb(f"st_cur{i}", [P, N * N], F32, sup) for i in range(2)]
        postb = sb("postb", [P, D], F32, sup)
        norm = sb("norm", [P, 4, 2], F32, sup)
        stats2 = sb("stats2", [P, T, 6], F32, sup)
        mv2 = sb("mv2", [P, T, 2], F32, sup)
        std2 = sb("std2", [P, 3, T], F32, sup)
        int_b = sb("int_b", [P, 2, 2, KD, D], F32, sup)
        prod = [sb(f"prod{i}", [P, N, 2, W_COLS], F32, sup) for i in range(2)]
        mag2 = [sb(f"mag2{i}", [P, N, W_COLS], F32, sup) for i in range(2)]
        zero.append(sb("zero1", [P, N, W_COLS], F32, sup))
        acc = sb("acc", [P, N, 2, W_COLS], F32, sup)
        gsum = sb("gsum", [P, N, W_COLS], F32, sup)
        sup_t = [sb(f"sup_t{i}", [P, 2, D], F32, sup) for i in range(2)]
        junk = sb("junk", [P, 2, D], F32, sup)
        meas = int_a[:, 0, :, :, :]
        meas_neg = int_a[:, 1, 0, :, :]
        post_wt = int_a[:, 1, 1, :, :]
        topz = int_b[:, 0, 0, :, :]
        sq = int_b[:, 0, 1, :, :]
        amp_T = int_b[:, 1, :, :, :]
        row_t = [at_t[t % 2][:, t // 2, :, :].rearrange("p k b -> p (k b)") for t in range(BT)]
        flat4 = "p n e d -> p (n e d)"
        z_out = [prod[hf][:, :, :, :].rearrange(flat4).rearrange("p (k b) -> p k b", k=KD) for hf in range(2)]
        part = z_t
        h1_T = acc[:, :, :, :].rearrange(flat4).rearrange("p (k b) -> p k b", k=KD)
        h2_T = gsum[:, :, :].rearrange("p n d -> p (n d)").rearrange("p (k b) -> p k b", k=2)
        top2_wt = mag2[0]
        y_row = mag2[1][0:1, :, :].rearrange("p n d -> p (n d)")

        consts_in = sem("consts_in")
        raw_in = [sem(f"raw_in{i}") for i in range(RAW)]
        x_in = [sem(f"x_in{i}") for i in range(U_X)]
        x_high = sem("x_high")
        x_split = sem("x_split")
        hi_done = sem("hi_done")
        split_done = sem("split_done")
        w_used = sem("w_used")
        b1_in = [sem(f"b1_in{i}") for i in range(2)]
        h_evac = sem("h_evac")
        bn_done = sem("bn_done")
        var_done = sem("var_done")
        std_done = sem("std_done")
        norm_step = sem("norm_step")
        ln_done = sem("ln_done")
        tr_done = sem("tr_done")
        gelu_done = sem("gelu_done")
        hT_high = sem("hT_high")
        hT_done = sem("hT_done")
        top_evac = sem("top_evac")
        s_evac = sem("s_evac")
        st_out = [sem(f"st_out{i}") for i in range(2)]

        s_high = sem("s_high")
        qk_mm = sem("qk_mm")
        qk_high = sem("qk_high")
        qk_low = sem("qk_low")
        neg_done = sem("neg_done")
        sc_mm = sem("sc_mm")
        sc_masked = sem("sc_masked")
        sc_sum = sem("sc_sum")
        soft = sem("soft")
        mag_done = sem("mag_done")
        exp_done = sem("exp_done")
        mask_in = sem("mask_in")
        u_moved = sem("u_moved")
        bv_in = sem("bv_in")
        v_mm = sem("v_mm")
        v_done = sem("v_done")
        wt_done = sem("wt_done")
        av_mm = sem("av_mm")
        o_high = sem("o_high")
        o_low = sem("o_low")
        wo_mm = sem("wo_mm")
        wo_evac = sem("wo_evac")
        at_out = [sem(f"at_out{i}") for i in range(4)]

        ids_in = sem("ids_in")
        emb_in = sem("emb_in")
        int_in = [sem(f"int_in{i}") for i in range(N)]
        at_in = [sem(f"at_in{i}") for i in range(2)]
        neg2 = sem("neg2")
        z_mm = sem("z_mm")
        z_evac = sem("z_evac")
        cur = sem("cur")
        sq_done = sem("sq_done")
        m_step = sem("m_step")
        rt_done = sem("rt_done")
        rc_done = sem("rc_done")
        u_done = sem("u_done")
        a_step = sem("a_step")
        ua_done = sem("ua_done")
        g_done = sem("g_done")
        g_step = sem("g_step")
        zg_done = sem("zg_done")
        pairs = sem("pairs")
        t_step = sem("t_step")
        nrm_sq = sem("nrm_sq")
        nrm_a = sem("nrm_a")
        nrm_rt = sem("nrm_rt")
        nrm_b = sem("nrm_b")
        st_mm = sem("st_mm")
        st_evac = sem("st_evac")
        fin_in = {x: sem(f"{x}_in") for x in ("meas", "post", "postb", "topz", "part0", "part1", "top2")}
        neg3 = sem("neg3")
        me_mm = sem("me_mm")
        me_sq = sem("me_sq")
        me_sum = sem("me_sum")
        amp = sem("amp")
        row_mm = sem("row_mm")
        row_in = sem("row_in")
        row_bn = sem("row_bn")
        row_mv = sem("row_mv")
        row_var = sem("row_var")
        row_std = sem("row_std")
        row_rstd = sem("row_rstd")
        row_ln = sem("row_ln")
        row_tr = sem("row_tr")
        z_gelu = sem("z_gelu")
        part_sum = sem("part_sum")
        t1_mm = sem("t1_mm")
        t1_sum = sem("t1_sum")
        t1_relu = sem("t1_relu")
        t2_mm = sem("t2_mm")
        t2_relu = sem("t2_relu")
        y_mm = sem("y_mm")
        y_done = sem("y_done")
        y_out = sem("y_out")

        def head_parts(m, slot):
            for half in range(2):
                hh = half ^ (m % 2)
                yield (q_t[slot][:, :, hh, :] if m in (Q_R, Q_I) else k_t[slot][:, :, hh, 0, :]), slice(HD * half, HD * half + HD)

        def col(base, n=1):
            return colt[:, base:base + n]

        def mm3(pe, out, lh, ll, rh, rl, start, stop):
            pe.matmul(out, ll, rh, start=start, stop=False)
            pe.matmul(out, lh, rl, start=False, stop=False)
            return pe.matmul(out, lh, rh, start=False, stop=stop)

        def stream_before(half, e):
            return U_X + half * U_HALF + e * U_PASS

        def stream_pos(half, e, u, late=False):
            extra = 0
            if e == 1 and late:
                extra = U_X
            elif e == 1 and isinstance(u, int):
                extra = min(max(u - X_FROM, 0), U_X)
            return stream_before(half, e) + u + extra

        block = ctx.enter_context(nc.Block())

        @block.sync
        def _(sp):
            for slot in range(RAW):
                sp.sem_inc(raw_in[slot], U_X // RAW * 16)

            def load(pos, src, slot):
                sp.wait_ge(split_done, pos - RAW + 1)
                sp.dma_start(raw[slot][:, :], src).then_inc(raw_in[slot], 16)

            with sp.Fori(0, HALVES) as half:
                for e in range(2):
                    fixed = X_FROM
                    with sp.Fori(0, fixed // RAW) as g:
                        for s in range(RAW):
                            load(stream_before(half, e) + g * RAW + s, w_units[e, g * RAW + s], s)
                    for u in range(fixed, fixed + 8):
                        pos = stream_pos(half, e, u)
                        k = (U_X + e * U_PASS + u + (u - fixed if e else 0)) % RAW
                        load(pos, w_units[e, u], k)
                        if e:
                            load(pos + 1, x_units[half + 1, u - fixed], (k + 1) % RAW)
                    with sp.Fori(fixed // RAW + 2, U_PASS // RAW) as g:
                        for s in range(RAW):
                            load(stream_before(half, e) + (U_X if e else 0) + g * RAW + s,
                                 w_units[e, g * RAW + s], s)

            def load_s(t):
                for u in range(RAW):
                    e, g = u // 2, u % 2
                    load(t * RAW + U_A + u,
                         s_T[e, bass.ds(t, 1), :, 2 * g:2 * g + 2, :, :].rearrange("o p k n b -> (o p) (k n b)"), u)

            for i in range(2):
                sp.wait_ge(st_out[i], 16 + 320)
            load_s(0)
            for i in range(2):
                sp.wait_ge(st_out[i], ST_A)
            sp.wait_ge(tr_done, 4 * KH)
            sp.dma_start(mask[:, :], mask_d).then_inc(mask_in, 16)
            with sp.Fori(1, T) as t:
                load_s(t)

            def load_sv(t, pos):
                for u in range(RAW):
                    e, g = u // 2, u % 2
                    load(pos + u, s_T[e, bass.ds(t, 1), :, 2 * g:2 * g + 2, :, :].rearrange("o p k n b -> (o p) (k n b)"), u)

            def store_at(t):
                for j in range(8):
                    sp.wait_ge(wo_evac, t * 8 + j + 1)
                    sp.dma_start(at_T[bass.ds(t, 1), :, :, j // 4, j % 4, :].rearrange("o n p b -> p (o n) b"),
                                 out_st[j % 4][:, :].rearrange("p (n b) -> p n b", n=N)).then_inc(at_out[j % 4], 16)

            load_sv(0, U_B)
            for u in range(U_X):
                if u == 4:
                    sp.wait_ge(qk_mm, 4 * CH)
                    sp.dma_start(bv_row[:, :, :].rearrange("p e d -> p (e d)"), bv.to_broadcast((P, 2 * D))).then_inc(bv_in, 16)
                load(U_B + RAW + u, x_units[3, u], u % RAW)
            load_sv(1, U_B + U_X + RAW)
            with sp.Fori(0, T - 2) as t:
                store_at(t)
                load_sv(t + 2, U_B + U_X + 2 * RAW + t * RAW)
            store_at(T - 2)

            def load_at(t, n):
                s = n % 2
                if not (isinstance(t, int) and t == 0 and n < 2):
                    sp.wait_ge(z_mm, t * 8 + 2 * n - 2)
                sp.dma_start(at_t[s][:, 0:2, :, :].rearrange("p e k b -> p (e k b)"),
                             at_T[bass.ds(t, 1), n, :, :, :, :].rearrange("o p e k b -> (o p) (e k b)")).then_inc(at_in[s], 16)

            sp.wait_ge(v_mm, 8 * T)
            sp.wait_ge(split_done, U_B + U_X + RAW * T)
            for i in range(4):
                sp.wait_ge(at_out[i], 16 + 2 * 16)
            for n in range(2):
                sp.dma_start(int_a[:, n, :, :, :].rearrange("p e k d -> p (e k d)"), int_w[n]).then_inc(int_in[n], 16)
                load_at(0, n)
            store_at(T - 1)
            sp.wait_ge(wo_mm, 8 * T)
            sp.wait_ge(av_mm, 2 + SUB * T)
            for i in range(4):
                sp.wait_ge(at_out[i], 16 + 2 * T * 16)
            for n in range(2, 4):
                sp.dma_start(int_b[:, n - 2, :, :, :].rearrange("p e k d -> p (e k d)"), int_w[n]).then_inc(int_in[n], 16)
            for n in range(2, 4):
                load_at(0, n)
            with sp.Fori(1, T) as t:
                for n in range(N):
                    load_at(t, n)

            sp.dma_start(postb[:, :], post_b.to_broadcast((P, D))).then_inc(fin_in["postb"], 16)
            sp.wait_ge(z_mm, 8 * T - 6)
            sp.dma_start(meas.rearrange("p e k d -> p (e k d)"), meas_w).then_inc(fin_in["meas"], 16)
            sp.wait_ge(z_mm, 8 * T - 4)
            sp.dma_start(post_wt.rearrange("p k d -> p (k d)"), post_w).then_inc(fin_in["post"], 16)
            sp.wait_ge(z_mm, 8 * T - 2)
            sp.dma_start(topz.rearrange("p k d -> p (k d)"), topz_w).then_inc(fin_in["topz"], 16)
            for hf in range(HALVES):
                sp.wait_ge(t_step, 4 * (T - 1 + hf))
                for e in range(2):
                    sp.dma_start(part[hf][:, :, e, :], top_part[e, :, :, hf * HB:hf * HB + HB].rearrange("c p b -> p c b")
                                 ).then_inc(fin_in[f"part{hf}"], 16)
            sp.dma_start(top2_wt[:, :, :].rearrange("p k d -> p (k d)"), top2_w).then_inc(fin_in["top2"], 16)
            sp.wait_ge(y_done, 2)
            sp.dma_start(y, y_row).then_inc(y_out, 16)
            sp.wait_ge(y_out, 16)

        @block.scalar
        def _(act):
            for s in range(2):
                act.sem_inc(st_out[s], 16)
            for u in range(U_X):
                act.dma_start(x_raw[:, 2 * u:2 * u + 2, :], x_units[0, u].rearrange("p (k b) -> p k b", k=2)).then_inc(x_in[u], 16)
            act.dma_start(colt[:, :], cols).then_inc(consts_in, 16)
            act.dma_start(ident[:, :], eye).then_inc(consts_in, 16)
            act.dma_start(ids_t[:, :], ids).then_inc(ids_in, 16)
            act.sem_inc(hi_done, U_X)

            def landed(pos, slot):
                act.wait_ge(raw_in[slot], (pos - slot) * 4 + 16)

            def high(half, e, u, static, late=False):
                pos = stream_pos(half, e, u, late)
                landed(pos, static % RAW)
                act.wait_ge(w_used, half * 2 * U_PASS + e * U_PASS + u - SPLIT + 1 + CREDIT_W)
                act.activation(w_hi[u_slot(u, static)][:, :], raw[static % RAW][:, :], ACT.Identity).then_inc(hi_done, 1)

            def u_slot(u, static):
                return static % SPLIT

            with act.Fori(0, HALVES) as half:
                for e in range(2):
                    def it(n):
                        return half * (2 * n) + e * n

                    def store_s(oc, n, kd, en=e):
                        act.wait_ge(s_evac, half * (2 * OC) + en * OC + oc + 2)
                        dst = s_T[en, bass.ds(half * BT, BT), :, kd, n, :].rearrange("t p b -> p t b")
                        act.dma_start(dst, stage[kd % 2][:, :].rearrange("p (t b) -> p t b", t=BT)).then_inc(st_out[kd % 2], 16)

                    def first_high(hp, store=False):
                        for par in range(2):
                            for j in range(8):
                                high(half, e, hp * 16 + par * 8 + j, par * 8 + j)
                                if j == 1 and par == 0 and store:
                                    store_s(OC - 1, N - 1, KD - 1, 0)
                                if j == 2:
                                    act.wait_ge(h_evac, it(4 * HC) + hp * 8 + par * 4 + 4)
                                    act.dma_start(b1row[par][:, :],
                                                  b1[e, bass.ds(hp * 1024 + par * 512, 512)].rearrange("(a n) -> a n", a=1).to_broadcast((P, 512))
                                                  ).then_inc(b1_in[par], 16)

                    if e == 0:
                        with act.Fori(0, HC // 2) as hp:
                            first_high(hp)
                    else:
                        first_high(0, store=True)
                        first_high(1)
                    u0 = U_ENC1
                    for j in range(3):
                        high(half, e, u0 + j, u0 + j)
                    act.wait_ge(var_done, it(1) + 1)
                    act.wait_ge(consts_in, 32)
                    act.activation(std[:, 1, :], std[:, 0, :], ACT.Sqrt).then_inc(std_done, 1)
                    high(half, e, u0 + 3, u0 + 3)
                    u2 = U_ENC1 + U_TOP
                    high(half, e, u2, u2)

                    def store_top(c):
                        act.wait_ge(top_evac, it(4) + c + 1)
                        act.dma_start(top_part[e, c, :, bass.ds(half * HB, HB)], stage[c % 2][:, :]).then_inc(st_out[c % 2], 16)

                    for k in range(KH):
                        act.wait_ge(tr_done, it(KH) + k + 1)
                        if k >= 2:
                            act.wait_ge(hT_done, it(KH) + k - 1)
                        act.activation(gel[k % 2][:, :], ps[:, 4 + k % 4, :], ACT.Gelu,
                                       scale=col(e * C_ENC + C_G + k), bias=col(e * C_ENC + C_BE + k)).then_inc(gelu_done, 1)
                        if k == 1:
                            high(half, e, u2 + 1, u2 + 1)
                        if k in (2, 4, 6, 8):
                            store_top(k // 2 - 1)
                        if k == 11:
                            high(half, e, u2 + 2, u2 + 2)
                    high(half, e, u2 + 3, u2 + 3)

                    store_s(0, 0, 0)
                    for oc in range(1, 8):
                        for v in range(2):
                            u = u2 + 2 * oc + 2 + v
                            if oc < 7:
                                st = (U_X + e * U_PASS + u + (min(max(u - u2 - 8, 0), 8) if e else 0))
                                pos = stream_pos(half, e, u)
                                landed(pos, st % RAW)
                                act.wait_ge(w_used, half * 2 * U_PASS + e * U_PASS + u - SPLIT + 1 + CREDIT_W)
                                act.activation(w_hi[u % SPLIT][:, :], raw[st % RAW][:, :], ACT.Identity).then_inc(hi_done, 1)
                                if e and u - u2 >= 8:
                                    xu = u - u2 - 8
                                    landed(pos + 1, (st + 1) % RAW)
                                    act.activation(x_hi[:, 2 * xu:2 * xu + 2, :],
                                                   raw[(st + 1) % RAW][:, :].rearrange("p (k b) -> p k b", k=2),
                                                   ACT.Identity).then_inc(hi_done, 1)
                        if oc < 7:
                            store_s(oc, oc // 4, oc % 4)
                    with act.Fori(2, OC // 4) as og:
                        for q in range(4):
                            for v in range(2):
                                high(half, e, u2 + og * 8 + 2 * q + v, u2 + 2 * q + v, True)
                            if q == 0:
                                store_s(og * 4 - 1, og - 1, KD - 1)
                            else:
                                store_s(og * 4 + q - 1, og, q - 1)
                    if e == 1:
                        store_s(OC - 1, N - 1, KD - 1)

            def high_s(t, slot):
                for e in range(2):
                    for kd in range(KD):
                        u = e * 2 + kd // 2
                        if kd % 2 == 0:
                            act.wait_ge(raw_in[u], t * 16 + (U_A // RAW + 1) * 16)
                            if not (isinstance(t, int) and t < 2):
                                act.wait_ge(qk_mm, t * 16 - 16)
                        src = raw[u][:, kd % 2 * 512:kd % 2 * 512 + 512].rearrange("p (n s b) -> p s n b", n=N, s=SUB)
                        act.activation(s_hi[slot][:, e, kd, :].rearrange("p (s n b) -> p s n b", n=N, s=SUB), src,
                                       ACT.Identity).then_inc(s_high, 1)

            def high_qk(g, c, slot):
                act.wait_ge(sc_mm, 4 * g + 4)
                for a, m in enumerate(ORDER):
                    act.wait_ge(qk_mm, 4 * g + a + 1)
                    for x, rows in head_parts(m, slot):
                        last = act.activation(x[rows, 0], ps[rows, a, :], ACT.Identity, bias=col(C_QKVO + m * KD + c)[rows])
                    last.then_inc(qk_high, 1)
                act.wait_ge(qk_low, 4 * g + 4 + 3)
                k = k_t[slot]
                act.activation(k[0:HD, :, :, 1, :], k[HD:P, :, :, 0, :].bitcast(F32), ACT.Copy, scale=-1.0)
                act.activation(k[HD:P, :, :, 1, :], k[0:HD, :, :, 0, :].bitcast(F32), ACT.Copy).then_inc(neg_done, 1)

            def score_tile(t, par, first=False):
                for c in range(KD):
                    high_qk(t * 4 + c, c, c % 2)
                    if c == 1:
                        high_s(t + 1, 1 - par)
                    if not first and c == 1:
                        act.wait_ge(soft, t * SOFT_STEPS - SOFT_STEPS + 2)
                        act.activation(mag[:, :, :], square[:, :, 0, :], ACT.Sqrt).then_inc(mag_done, 1)
                    if not first and c == 2:
                        act.wait_ge(soft, t * SOFT_STEPS - SOFT_STEPS + 4)
                        act.activation(mag[:, :, :], mag[:, :, :], ACT.Exp, scale=HD ** -0.5).then_inc(exp_done, 1)

            act.wait_ge(tr_done, 4 * KH)
            act.wait_ge(w_used, CREDIT_W + 4 * U_PASS)
            high_s(0, 0)
            score_tile(0, 0, first=True)
            with act.Fori(0, 3) as i:
                score_tile(2 * i + 1, 1)
                score_tile(2 * i + 2, 0)
            score_tile(T - 1, 1)
            for s in range(4):
                act.sem_inc(at_out[s], 16)

            def high_vo(u):
                act.wait_ge(qk_mm, 4 * CH)
                act.wait_ge(raw_in[u % RAW], ((U_B + RAW + u) // RAW + 1) * 16)
                act.activation(x_hi[:, 2 * u:2 * u + 2, :], raw[u % RAW][:, :].rearrange("p (k b) -> p k b", k=2),
                               ACT.Identity).then_inc(hi_done, 1)

            for u in range(4):
                high_vo(u)
            act.wait_ge(soft, T * SOFT_STEPS - SOFT_STEPS + 2)
            act.activation(mag[:, :, :], square[:, :, 0, :], ACT.Sqrt).then_inc(mag_done, 1)
            act.wait_ge(soft, T * SOFT_STEPS - SOFT_STEPS + 4)
            act.activation(mag[:, :, :], mag[:, :, :], ACT.Exp, scale=HD ** -0.5).then_inc(exp_done, 1)
            for u in range(4, U_X):
                high_vo(u)

            def high_sv(t, e, kd):
                u = e * 2 + kd // 2
                if kd % 2 == 0:
                    act.wait_ge(raw_in[u], t * 16 + ((U_B + U_X) // RAW + 1) * 16)
                src = raw[u][:, kd % 2 * 512:kd % 2 * 512 + 512].rearrange("p (n s b) -> p s n b", n=N, s=SUB)
                act.activation(s_hi[0][:, e, kd, :].rearrange("p (s n b) -> p s n b", n=N, s=SUB), src,
                               ACT.Identity).then_inc(s_high, 1)

            def high_o(q, sub):
                act.wait_ge(av_mm, 2 + q + 1)
                b = 4 + sub % 2 * 2
                for e in range(2):
                    for hh in range(2):
                        act.activation(o_hi[HD * hh:HD * hh + HD, e, :, sub * P:sub * P + P],
                                       ps[HD * e:HD * e + HD, b:b + 2, :].rearrange("p k (c z q) -> p (k c) z q", c=2, z=2)[:, :, hh, :],
                                       ACT.Identity).then_inc(o_high, 1)

            def value_tile(t, last=False):
                for sub in range(SUB):
                    high_o(t * 4 + sub, sub)
                for j in range(8):
                    act.wait_ge(wo_mm, t * 8 + j + 1)
                    act.wait_ge(at_out[j % 4], t * 32 + j // 4 * 16 + 16)
                    act.activation(out_st[j % 4][:, :].rearrange("p (n s b) -> p s n b", n=N, s=SUB),
                                   ps[:, j % 4, :].rearrange("p (s n b) -> p s n b", n=N, s=SUB), ACT.Identity,
                                   bias=col(C_QKVO + O_R * KD + j)).then_inc(wo_evac, 1)
                    if not last:
                        if j == 0:
                            act.wait_ge(v_mm, t * 8 + 8)
                        high_sv(t + 1, j // 4, j % 4)

            value_tile(0)
            with act.Fori(1, T - 1) as t:
                value_tile(t)
            value_tile(T - 1, last=True)

            def half(f):
                return slice(f % 2 * W_COLS, f % 2 * W_COLS + W_COLS)

            def squares(f, q, t):
                act.wait_ge(z_evac, t * 8 + 8)
                if not (isinstance(f, int) and f < 2):
                    act.wait_ge(t_step, f * 2 - 2)
                act.activation(prod[q % 2][:, :, :, :].rearrange("p n e d -> p (n e) d"),
                               z_t[q // 2 % 2][:, :, :, half(q)].rearrange("p n e d -> p (n e) d"), ACT.Square).then_inc(sq_done, 1)

            def roots(f, q):
                act.wait_ge(m_step, f * 2 + 2)
                act.activation(mag2[q % 2][:, :, :], mag2[q % 2][:, :, :], ACT.Sqrt).then_inc(rt_done, 1)

            def norm_squares(t, q):
                act.wait_ge(t_step, t * 4 + 4)
                if not (isinstance(t, int) and t == 0):
                    act.wait_ge(nrm_sq, t)
                act.activation(junk[:, :, :], sup_t[q // 2 % 2][:, :, :], ACT.Square, accum_out=norm[:, 0, q // 2 % 2:q // 2 % 2 + 1]).then_inc(nrm_sq, 1)

            def norm_root(t, q):
                act.wait_ge(nrm_a, t + 1)
                act.activation(norm[:, 2, q // 2 % 2:q // 2 % 2 + 1], norm[:, 1, q // 2 % 2:q // 2 % 2 + 1], ACT.Sqrt).then_inc(nrm_rt, 1)

            def evac_sup(t):
                for e in range(2):
                    act.wait_ge(st_mm, t * 2 + e + 1)
                    act.activation(sup_T[:, e, :, bass.ds(t * P, P)], ps[:, 6 + e, :].rearrange("p (k b) -> p k b", k=KD),
                                   ACT.Identity).then_inc(st_evac, 1)

            def evac_z(t, par, n):
                for e in range(2):
                    act.wait_ge(z_mm, t * 8 + 2 * n + e + 1)
                    if not (isinstance(t, int) and t < 2):
                        act.wait_ge(zg_done, t * 2 - 2)
                    act.activation(z_t[par][:, n, e, :], ps[:, n % 2 * 2 + e, :], ACT.Identity).then_inc(z_evac, 1)

            def negate(t, n):
                act.wait_ge(at_in[n % 2], t * 32 + n // 2 * 16 + 16)
                act.activation(at_t[n % 2][:, 2, :, :], at_t[n % 2][:, 1, :, :], ACT.Copy, scale=-1.0).then_inc(neg2, 1)

            def sup_tile(t, par):
                now = isinstance(t, int)
                q = 2 * (1 - par)
                if not now or t >= 1:
                    squares(2 * t - 2, q, t - 1)
                    roots(2 * t - 2, q)
                if not (now and t == 0):
                    negate(t, 1)
                evac_z(t, par, 0)
                negate(t, 2)
                evac_z(t, par, 1)
                if not now or t >= 1:
                    squares(2 * t - 1, q + 1, t - 1)
                if not now or t >= 2:
                    norm_squares(t - 2, 2 * par)
                if not now or t >= 1:
                    roots(2 * t - 1, q + 1)
                if not now or t >= 2:
                    norm_root(t - 2, 2 * par)
                negate(t, 3)
                evac_z(t, par, 2)
                if not (now and t == T - 1):
                    negate(t + 1, 0)
                evac_z(t, par, 3)
                if not now or t >= 2:
                    evac_sup(t - 2)

            negate(0, 0)
            negate(0, 1)
            sup_tile(0, 0)
            sup_tile(1, 1)
            with act.Fori(1, T // 2 - 1) as i:
                sup_tile(2 * i, 0)
                sup_tile(2 * i + 1, 1)
            sup_tile(T - 2, 0)
            sup_tile(T - 1, 1)

            def measured_squares(hf, c):
                g = hf * KD + c
                act.wait_ge(me_mm, g + 1)
                if g >= 2:
                    act.wait_ge(me_sum, g - 1)
                for e in range(2):
                    act.activation(sq[:, c % 2 * 2 + e, :], ps[:, c % 2 * 2 + e, :], ACT.Square).then_inc(me_sq, 1)

            def amplitude(hf, c):
                act.wait_ge(me_sum, hf * KD + c + 1)
                act.activation(amp_T[:, hf, c, :], amp_T[:, hf, c, :], ACT.Sqrt).then_inc(amp, 1)

            def row_root(t):
                act.wait_ge(row_var, t + 1)
                act.activation(std2[:, 1, t:t + 1], std2[:, 0, t:t + 1], ACT.Sqrt).then_inc(row_std, 1)

            def row_gelu(t):
                act.wait_ge(row_tr, t + 1)
                for k in range(KD):
                    act.activation(z_out[t // BT][:, k, t % BT * P:t % BT * P + P], ps[:, 6 + t % 2, k * P:k * P + P], ACT.Gelu,
                                   bias=col(C_POST + KD + k), scale=col(C_POST + k)).then_inc(z_gelu, 1)

            def relu_1(hf):
                for c in range(KD):
                    act.wait_ge(t1_sum, hf * KD + c + 1)
                    act.activation(h1_T[:, c, :], h1_T[:, c, :], ACT.Relu, bias=col(C_TOP1 + c)).then_inc(t1_relu, 1)

            def relu_2(hf):
                for c in range(2):
                    act.wait_ge(t2_mm, hf * 2 + c + 1)
                    act.activation(h2_T[:, c, :], ps[:, 4 + c, :], ACT.Relu, bias=col(C_TOP2 + c)).then_inc(t2_relu, 1)

            def result(hf):
                act.wait_ge(y_mm, hf + 1)
                act.activation(y_row[:, hf * HB:hf * HB + HB], ps[0:1, 6, :], ACT.Identity).then_inc(y_done, 1)

            act.wait_ge(fin_in["meas"], 16)
            act.wait_ge(z_mm, 8 * T - 4)
            act.activation(meas_neg, meas[:, 1, :, :], ACT.Copy, scale=-1.0).then_inc(neg3, 1)
            squares(STEPS - 2, 2, T - 1)
            roots(STEPS - 2, 2)
            measured_squares(0, 0)
            squares(STEPS - 1, 3, T - 1)
            norm_squares(T - 2, 0)
            roots(STEPS - 1, 3)
            norm_root(T - 2, 0)
            measured_squares(0, 1)
            evac_sup(T - 2)
            amplitude(0, 0)
            measured_squares(0, 2)
            amplitude(0, 1)
            measured_squares(0, 3)
            amplitude(0, 2)
            amplitude(0, 3)
            norm_squares(T - 1, 2)
            norm_root(T - 1, 2)
            evac_sup(T - 1)
            row_root(0)
            row_root(1)
            measured_squares(1, 0)
            row_root(2)
            row_root(3)
            row_gelu(0)
            row_gelu(1)
            measured_squares(1, 1)
            amplitude(1, 0)
            row_gelu(2)
            row_gelu(3)
            amplitude(1, 1)
            measured_squares(1, 2)
            amplitude(1, 2)
            measured_squares(1, 3)
            amplitude(1, 3)
            relu_1(0)
            for t in range(BT, T):
                row_root(t)
            relu_2(0)
            for t in range(BT, T):
                row_gelu(t)
            result(0)
            relu_1(1)
            relu_2(1)
            result(1)

        @block.gpsimd
        def _(pool):
            def low(pos, slot, lo, hi):
                pool.wait_ge(hi_done, pos + 1)
                pool.tensor_tensor(lo, raw[slot][:, :].rearrange("p (k b) -> p k b", k=2) if len(lo.shape) == 3 else raw[slot][:, :],
                                   hi.bitcast(F32), ALU.subtract).then_inc(split_done, 1)

            def low_x(pos, slot, u):
                low(pos, slot, x_lo[:, 2 * u:2 * u + 2, :], x_hi[:, 2 * u:2 * u + 2, :])

            pool.sem_inc(split_done, U_X)
            with pool.Fori(0, HALVES) as half:
                for e in range(2):
                    fixed = X_FROM
                    with pool.Fori(0, fixed // RAW) as g:
                        for s in range(RAW):
                            low(stream_before(half, e) + g * RAW + s, s, w_lo[s % SPLIT][:, :], w_hi[s % SPLIT][:, :])
                    for u in range(fixed, fixed + 8):
                        pos = stream_pos(half, e, u)
                        k = (U_X + e * U_PASS + u + (u - fixed if e else 0)) % RAW
                        low(pos, k, w_lo[u % SPLIT][:, :], w_hi[u % SPLIT][:, :])
                        if e:
                            low_x(pos + 1, (k + 1) % RAW, u - fixed)
                    with pool.Fori(fixed // RAW + 2, U_PASS // RAW) as g:
                        for s in range(RAW):
                            low(stream_before(half, e) + (U_X if e else 0) + g * RAW + s, s,
                                w_lo[s % SPLIT][:, :], w_hi[s % SPLIT][:, :])

            def low_s(t, slot):
                for e in range(2):
                    for kd in range(KD):
                        u = e * 2 + kd // 2
                        pool.wait_ge(s_high, t * 8 + e * 4 + kd + 1)
                        src = raw[u][:, kd % 2 * 512:kd % 2 * 512 + 512].rearrange("p (n s b) -> p s n b", n=N, s=SUB)
                        low = pool.tensor_tensor(s_lo[slot][:, e, kd, :].rearrange("p (s n b) -> p s n b", n=N, s=SUB), src,
                                                 s_hi[slot][:, e, kd, :].bitcast(F32).rearrange("p (s n b) -> p s n b", n=N, s=SUB),
                                                 ALU.subtract)
                        if kd % 2:
                            low.then_inc(split_done, 1)

            low_s(0, 0)
            with pool.Fori(0, 3) as i:
                low_s(2 * i + 1, 1)
                low_s(2 * i + 2, 0)
            low_s(7, 1)
            low_s(8, 0)
            for u in range(4):
                low_x(U_A + u, u % RAW, u)

            def wide(q, t, sub):
                pool.wait_ge(av_mm, q + 1)
                src = u_t[:, t, sub, :] if isinstance(t, int) else u_t[:, bass.ds(t, 1), sub, :].rearrange("p o x -> p (o x)")
                pool.tensor_tensor(wt[sub % 2][:, :, :].rearrange("p h (n b) -> p (h n) b", n=N),
                                   src.unsqueeze(2).to_broadcast((P, H * N, 32)),
                                   mask[:, :].unsqueeze(1).to_broadcast((P, H * N, 32)), ALU.mult).then_inc(wt_done, 1)

            def low_sv(t):
                for e in range(2):
                    for kd in range(KD):
                        u = e * 2 + kd // 2
                        pool.wait_ge(s_high, t * 8 + 8 * T + e * 4 + kd + 1)
                        src = raw[u][:, kd % 2 * 512:kd % 2 * 512 + 512].rearrange("p (n s b) -> p s n b", n=N, s=SUB)
                        low = pool.tensor_tensor(s_lo[0][:, e, kd, :].rearrange("p (s n b) -> p s n b", n=N, s=SUB), src,
                                                 s_hi[0][:, e, kd, :].bitcast(F32).rearrange("p (s n b) -> p s n b", n=N, s=SUB),
                                                 ALU.subtract)
                        if kd % 2:
                            low.then_inc(split_done, 1)

            pool.wait_ge(u_moved, 16)
            wide(0, 0, 0)
            wide(1, 0, 1)
            for u in range(4, U_X):
                low_x(U_A + u, u % RAW, u)
            wide(2, 0, 2)
            wide(3, 0, 3)
            pool.wait_ge(u_moved, 32)
            with pool.Fori(1, T) as t:
                low_sv(t)
                for sub in range(SUB):
                    wide(t * 4 + sub, t, sub)

            pool.wait_ge(ids_in, 16)
            for t in range(T):
                for i in range(N):
                    pool.indirect_dma_start(out=strength[:, t, i * N:i * N + N], out_offset=None, in_=tbls[i],
                                            in_offset=bass.IndirectOffsetOnAxis(ap=ids_t[:, t * N + i:t * N + i + 1], axis=0)
                                            ).then_inc(emb_in, 16)

            def half(f):
                return slice(f % 2 * W_COLS, f % 2 * W_COLS + W_COLS)

            def phasors(f, q):
                pool.wait_ge(rc_done, f + 1)
                z = z_t[q // 2 % 2][:, :, :, half(q)]
                for e in range(2):
                    last = pool.tensor_tensor(prod[q % 2][:, :, e, :], z[:, :, e, :], mag2[q % 2][:, :, :], ALU.mult)
                last.then_inc(u_done, 1)

            def weighted(f, q):
                pool.wait_ge(g_step, f * 12 + 12)
                z = z_t[q // 2 % 2][:, :, :, half(q)]
                for e in range(2):
                    last = pool.tensor_tensor(prod[q % 2][:, :, e, :], z[:, :, e, :], gsum[:, :, :], ALU.mult)
                last.then_inc(zg_done, 1)
                pool.wait_ge(zg_done, f + 1)
                flat = "p n e d -> p (n e d)"
                pool.tensor_tensor(prod[q % 2][:, 0:2, :, :].rearrange(flat), prod[q % 2][:, 0:2, :, :].rearrange(flat),
                                   prod[q % 2][:, 2:4, :, :].rearrange(flat), ALU.add).then_inc(pairs, 1)

            def cosines(f, q):
                pool.wait_ge(a_step, f * 16 + 16)
                flat = "p n e d -> p (n e d)"
                pool.tensor_tensor(acc[:, :, :, :].rearrange(flat), acc[:, :, :, :].rearrange(flat),
                                   prod[q % 2][:, :, :, :].rearrange(flat), ALU.mult).then_inc(ua_done, 1)
                pool.wait_ge(ua_done, f + 1)
                if not (isinstance(f, int) and f == 0):
                    pool.wait_ge(zg_done, f)
                pool.tensor_tensor(gsum[:, :, :], acc[:, :, 0, :], acc[:, :, 1, :], ALU.add).then_inc(g_done, 1)

            def sup_tile(t, par, first=False):
                for z in range(2):
                    f, q = 2 * t + z, 2 * par + z
                    phasors(f, q)
                    if not (first and z == 0):
                        weighted(f - 1, (q - 1) % 4)
                    cosines(f, q)

            sup_tile(0, 0, first=True)
            sup_tile(1, 1)
            with pool.Fori(1, T // 2 - 1) as i:
                sup_tile(2 * i, 0)
                sup_tile(2 * i + 1, 1)
            sup_tile(T - 2, 0)
            sup_tile(T - 1, 1)
            weighted(STEPS - 1, 3)
            for hf in range(HALVES):
                pool.wait_ge(fin_in[f"part{hf}"], 32)
                pool.tensor_tensor(part[hf][:, :, 0, :], part[hf][:, :, 0, :], part[hf][:, :, 1, :], ALU.add).then_inc(part_sum, 1)

        @block.vector
        def _(dve):
            def split_hidden(dve, it, k):
                dve.wait_ge(gelu_done, it(KH) + k + 1)
                dve.tensor_copy(hT_hi[:, k, :], gel[k % 2][:, :]).then_inc(hT_high, 1)
                dve.wait_ge(hT_high, it(KH) + k + 1)
                dve.tensor_tensor(hT_lo[:, k, :], gel[k % 2][:, :], hT_hi[:, k, :].bitcast(F32), ALU.subtract).then_inc(hT_done, 1)

            dve.sem_inc(h_evac, CREDIT_H)
            dve.sem_inc(s_evac, 1)
            for u in range(U_X):
                x = slice(2 * u, 2 * u + 2)
                dve.wait_ge(x_in[u], 16)
                dve.tensor_copy(x_hi[:, x, :], x_raw[:, x, :]).then_inc(x_high, 1)
                dve.wait_ge(x_high, u + 1)
                dve.tensor_tensor(x_lo[:, x, :], x_raw[:, x, :], x_hi[:, x, :].bitcast(F32), ALU.subtract).then_inc(x_split, 1)
            dve.wait_ge(consts_in, 32)
            with dve.Fori(0, HALVES) as half:
                for e in range(2):
                    def it(n):
                        return half * (2 * n) + e * n

                    for hc in range(HC):
                        dve.wait_ge(w_used, it(U_PASS) + CREDIT_W + 8 * hc + 8)
                        dve.wait_ge(b1_in[hc % 2], it(HC // 2 * 16) + (hc // 2 + 1) * 16)
                        for bt in range(BT):
                            dve.tensor_tensor(h[:, bt, hc * 512:hc * 512 + 512], ps[:, (hc % 2) * 4 + bt, :],
                                              b1row[hc % 2][:, :], ALU.add).then_inc(h_evac, 1)
                        for bt in range(BT):
                            dve.wait_ge(h_evac, it(4 * HC) + CREDIT_H + 4 * hc + bt + 1)
                            dve.bn_stats(stats[:, bt, hc, :], h[:, bt, hc * 512:hc * 512 + 512]).then_inc(bn_done, 1)
                    dve.wait_ge(bn_done, it(BT * HC) + BT * HC)
                    dve.memset(std[:, 0, :], EPS).then_inc(norm_step, 1)
                    for bt in range(BT):
                        dve.bn_aggr(meanvar[:, bt, :], stats[:, bt, :, :].rearrange("p c s -> p (c s)")).then_inc(norm_step, 1)
                    dve.wait_ge(norm_step, it(BT + 2) + BT + 1)
                    dve.tensor_tensor(std[:, 0, :], meanvar[:, :, 1], std[:, 0, :], ALU.add).then_inc(var_done, 1)
                    dve.wait_ge(std_done, it(1) + 1)
                    dve.reciprocal(std[:, 2, :], std[:, 1, :]).then_inc(norm_step, 1)
                    dve.wait_ge(norm_step, it(BT + 2) + BT + 2)
                    for bt in range(BT):
                        dve.tensor_scalar(h[:, bt, :], h[:, bt, :], meanvar[:, bt, 0:1], std[:, 2, bt:bt + 1],
                                          ALU.subtract, ALU.mult).then_inc(ln_done, 1)

                    split_hidden(dve, it, 0)
                    split_hidden(dve, it, 1)
                    dve.wait_ge(w_used, it(U_PASS) + CREDIT_W + U_ENC1 + U_TOP)
                    for c in range(4):
                        dve.wait_ge(st_out[c % 2], it(160) + (c // 2) * 16 + 16)
                        dve.tensor_copy(stage[c % 2][:, :], ps[:, c, :]).then_inc(top_evac, 1)
                        if c == 1:
                            for k in range(2, 6):
                                split_hidden(dve, it, k)
                    for k in range(6, KH):
                        split_hidden(dve, it, k)

                    for oc in range(OC):
                        dve.wait_ge(w_used, it(U_PASS) + CREDIT_W + U_ENC1 + U_TOP + 2 * oc + 2)
                        dve.wait_ge(st_out[oc % 2], it(160) + (oc // 2 + 3) * 16)
                        dve.tensor_scalar(stage[oc % 2][:, :], ps[:, oc % 4, :], col(e * C_ENC + C_B2 + oc), None,
                                          ALU.add).then_inc(s_evac, 1)

            dve.sem_inc(qk_low, 4)
            dve.sem_inc(sc_masked, 4)
            for i in range(2):
                dve.wait_ge(st_out[i], ST_A)
            dve.wait_ge(mask_in, 16)

            def low_qk(g, c, slot):
                for a, m in enumerate(ORDER):
                    dve.wait_ge(qk_high, 4 * g + a + 1)
                    for x, rows in head_parts(m, slot):
                        last = dve.scalar_tensor_tensor(out=x[rows, 1], in0=ps[rows, a, :], scalar=col(C_QKVO + m * KD + c)[rows],
                                                        in1=x[rows, 0].bitcast(F32), op0=ALU.add, op1=ALU.subtract)
                    last.then_inc(qk_low, 1)

            def own_scores(g, c, slot):
                for p in range(2):
                    if p or not (isinstance(g, int) and g == 0):
                        dve.wait_ge(sc_sum, 2 * g + p)
                    for b in range(2):
                        dve.wait_ge(sc_mm, 8 + 4 * g + 2 * p + b + 1)
                        dve.tensor_tensor(masked[:, b, :].rearrange("p (g r) -> p g r", r=32),
                                          ps[:, 4 + 2 * p + b, :].rearrange("p (g r) -> p g r", r=32),
                                          mask[:, :].unsqueeze(1).to_broadcast((P, 16, 32)), ALU.mult).then_inc(sc_masked, 1)
                    dve.wait_ge(sc_masked, 4 + 4 * g + 2 * p + 2)
                    dve.tensor_reduce(score[slot][:, c * 8 + 4 * p:c * 8 + 4 * p + 4, :, :].rearrange("p i a m -> p (i a m)"),
                                      masked[:, :, :].rearrange("p b (g r) -> p (b g) r", r=32), AX.X, ALU.add).then_inc(sc_sum, 1)

            def softmax_a(t, slot):
                base = t * SOFT_STEPS
                dve.wait_ge(sc_sum, t * 8 + 8)
                dve.tensor_tensor(square[:, :, :, :], score[slot][:, :, :, :], score[slot][:, :, :, :], ALU.mult).then_inc(soft, 1)
                dve.wait_ge(soft, base + 1)
                dve.scalar_tensor_tensor(out=square[:, :, 0, :], in0=square[:, :, 0, :], scalar=1e-8,
                                         in1=square[:, :, 1, :], op0=ALU.add, op1=ALU.add).then_inc(soft, 1)

            def softmax_b(t):
                base = t * SOFT_STEPS
                dve.wait_ge(mag_done, t + 1)
                dve.tensor_reduce(red[:, 0, :], mag[:, :, :], AX.X, ALU.max).then_inc(soft, 1)
                dve.wait_ge(soft, base + 3)
                dve.tensor_tensor(mag[:, :, :], mag[:, :, :], red[:, 0, :].unsqueeze(2).to_broadcast((P, H * SUB, N)),
                                  ALU.subtract).then_inc(soft, 1)

            def softmax_c(t):
                base = t * SOFT_STEPS
                dve.wait_ge(exp_done, t + 1)
                dve.tensor_reduce(red[:, 1, :], mag[:, :, :], AX.X, ALU.add).then_inc(soft, 1)
                dve.wait_ge(soft, base + 5)
                dve.reciprocal(red[:, 2, :], red[:, 1, :]).then_inc(soft, 1)
                dve.wait_ge(soft, base + 6)
                dst = probs[:, t, :, :] if isinstance(t, int) else probs[:, bass.ds(t, 1), :, :].rearrange("p o i m -> p (o i) m")
                dve.tensor_tensor(dst, mag[:, :, :], red[:, 2, :].unsqueeze(2).to_broadcast((P, H * SUB, N)),
                                  ALU.mult).then_inc(soft, 1)

            def score_tile(t, par, first=False):
                for c in range(KD):
                    low_qk(t * 4 + c, c, c % 2)
                    if not (first and c == 0):
                        own_scores(t * 4 + c - 1, (c - 1) % 4, par if c else 1 - par)
                    if not first:
                        if c == 0:
                            softmax_a(t - 1, 1 - par)
                        if c == 1:
                            softmax_b(t - 1)
                        if c == 2:
                            softmax_c(t - 1)

            score_tile(0, 0, first=True)
            with dve.Fori(0, 3) as i:
                score_tile(2 * i + 1, 1)
                score_tile(2 * i + 2, 0)
            score_tile(7, 1)
            own_scores(CH - 1, 3, 1)

            def turn_probs(t):
                for n in range(N):
                    for m in range(N):
                        dve.tensor_copy(u_t[32 * m:32 * m + 32, t, :, :].rearrange("p t s (h n) -> p t s h n", n=N)[:, :, :, :, n],
                                        probs[32 * n:32 * n + 32, t, :, m].rearrange("p t (h s) -> p t s h", s=SUB)).then_inc(u_moved, 1)

            dve.wait_ge(soft, (T - 1) * SOFT_STEPS)
            turn_probs(slice(0, T - 1))
            softmax_a(7, 1)
            softmax_b(7)
            softmax_c(7)
            dve.wait_ge(soft, T * SOFT_STEPS)
            turn_probs(slice(T - 1, T))

            def values_out(q, sub):
                for e in range(2):
                    dve.wait_ge(v_mm, 2 * q + e + 1)
                    dve.wait_ge(av_mm, q + 1)
                    dve.tensor_tensor(v_t[sub % 2][:, :, e, :], ps[:, sub % 2 * 2 + e, :].rearrange("p (h d) -> p h d", h=H),
                                      bv_row[:, e, :].rearrange("p (h d) -> p h d", h=H), ALU.add).then_inc(v_done, 1)

            def low_o(q, sub):
                b = 4 + sub % 2 * 2
                for e in range(2):
                    for hh in range(2):
                        rows = slice(HD * hh, HD * hh + HD)
                        dve.wait_ge(o_high, 4 * q + 2 * e + 2)
                        dve.tensor_tensor(o_lo[rows, e, :, sub * P:sub * P + P],
                                          ps[HD * e:HD * e + HD, b:b + 2, :].rearrange("p k (c z q) -> p (k c) z q", c=2, z=2)[:, :, hh, :],
                                          o_hi[rows, e, :, sub * P:sub * P + P].bitcast(F32), ALU.subtract).then_inc(o_low, 1)

            def value_tile(t, first=False):
                for sub in range(SUB):
                    values_out(t * 4 + sub, sub)
                    if sub:
                        low_o(t * 4 + sub - 1, sub - 1)
                low_o(t * 4 + 3, 3)

            dve.wait_ge(bv_in, 16)
            value_tile(0)
            with dve.Fori(1, T) as t:
                value_tile(t)

            def magnitudes(f, q):
                s = q % 2
                dve.wait_ge(sq_done, f + 1)
                dve.scalar_tensor_tensor(out=mag2[s][:, :, :], in0=prod[s][:, :, 0, :], scalar=TINY, in1=prod[s][:, :, 1, :],
                                         op0=ALU.max, op1=ALU.add).then_inc(m_step, 1)
                dve.wait_ge(m_step, f * 2 + 1)
                dve.tensor_scalar(zero[s][:, :, :], mag2[s][:, :, :], TINY, None, ALU.is_le).then_inc(m_step, 1)

            def reciprocals(f, q):
                s = q % 2
                dve.wait_ge(rt_done, f + 1)
                dve.reciprocal(mag2[s][:, :, :], mag2[s][:, :, :]).then_inc(rc_done, 1)

            def strengths(t, par):
                dve.wait_ge(emb_in, 16 * N * T)
                if not (isinstance(t, int) and t < 2):
                    dve.wait_ge(g_step, t * 24 - 24)
                src = strength[:, bass.ds(t, 1), :].rearrange("p o x -> p (o x)")
                dve.tensor_copy(st_cur[par][:, :], src).then_inc(cur, 1)

            def sums(f, q):
                par, s = q // 2 % 2, q % 2
                dve.wait_ge(u_done, f + 1)
                if not (isinstance(f, int) and f == 0):
                    dve.wait_ge(g_done, f)
                dve.wait_ge(cur, (f - s) // 2 + 1 if isinstance(f, int) else tile_of[0] + 1)
                for i in range(N):
                    for j in range(N):
                        st = st_cur[par][:, i * N + j:i * N + j + 1]
                        u = prod[s][:, i, :, :].rearrange("p e d -> p (e d)")
                        a = acc[:, j, :, :].rearrange("p e d -> p (e d)")
                        if i == 0:
                            dve.tensor_scalar(a, u, st, None, ALU.mult).then_inc(a_step, 1)
                        else:
                            dve.wait_ge(a_step, f * 16 + 4 * (i - 1) + j + 1)
                            dve.scalar_tensor_tensor(out=a, in0=u, scalar=st, in1=a, op0=ALU.mult, op1=ALU.add).then_inc(a_step, 1)

            def vanished(f, q):
                par, s = q // 2 % 2, q % 2
                dve.wait_ge(g_done, f + 1)
                for d in range(1, N):
                    for j in range(N):
                        i = (j + d) % N
                        if d > 1:
                            dve.wait_ge(g_step, f * 12 + 4 * (d - 2) + j + 1)
                        dve.scalar_tensor_tensor(out=gsum[:, j, :], in0=zero[s][:, i, :], scalar=st_cur[par][:, i * N + j:i * N + j + 1],
                                                 in1=gsum[:, j, :], op0=ALU.mult, op1=ALU.add).then_inc(g_step, 1)

            def total(f, q):
                par, s = q // 2 % 2, q % 2
                cols_ = slice(s * W_COLS, s * W_COLS + W_COLS)
                dve.wait_ge(pairs, f + 1)
                if not (isinstance(f, int) and f < 4):
                    dve.wait_ge(st_mm, tile_of[1] * 2 - 2)
                dve.tensor_tensor(sup_t[par][:, :, cols_], prod[s][:, 0, :, :], prod[s][:, 1, :, :], ALU.add).then_inc(t_step, 2)

            def norm_eps(t, par):
                dve.wait_ge(nrm_sq, t + 1)
                dve.tensor_scalar(norm[:, 1, par:par + 1], norm[:, 0, par:par + 1], 1e-8, None, ALU.add).then_inc(nrm_a, 1)

            def norm_rows(t, par):
                dve.wait_ge(nrm_rt, t + 1)
                dve.reciprocal(norm[:, 3, par:par + 1], norm[:, 2, par:par + 1]).then_inc(nrm_b, 1)
                dve.wait_ge(nrm_b, t * 2 + 1)
                dve.tensor_scalar(sup_t[par][:, :, :], sup_t[par][:, :, :], norm[:, 3, par:par + 1], None, ALU.mult).then_inc(nrm_b, 1)

            tile_of = [0, 0]

            def amplitude_sum(hf, c):
                dve.wait_ge(me_sq, (hf * KD + c + 1) * 2)
                dve.tensor_tensor(amp_T[:, hf, c, :], sq[:, c % 2 * 2, :], sq[:, c % 2 * 2 + 1, :], ALU.add).then_inc(me_sum, 1)

            def row_stats(t):
                dve.wait_ge(row_mm, t + 1)
                if t == 0:
                    dve.wait_ge(fin_in["postb"], 16)
                if t >= BT:
                    dve.wait_ge(row_tr, t - BT + 1)
                dve.tensor_tensor(row_t[t % BT], ps[:, 4 + t % 2, :], postb[:, :], ALU.add).then_inc(row_in, 1)
                dve.wait_ge(row_in, t + 1)
                dve.bn_stats(stats2[:, t, :], row_t[t % BT]).then_inc(row_bn, 1)
                dve.wait_ge(row_bn, t + 1)
                dve.bn_aggr(mv2[:, t, :], stats2[:, t, :]).then_inc(row_mv, 1)
                dve.wait_ge(row_mv, t + 1)
                dve.tensor_scalar(std2[:, 0, t:t + 1], mv2[:, t, 1:2], EPS, None, ALU.add).then_inc(row_var, 1)

            def row_norm(t):
                dve.wait_ge(row_std, t + 1)
                dve.reciprocal(std2[:, 2, t:t + 1], std2[:, 1, t:t + 1]).then_inc(row_rstd, 1)
                dve.wait_ge(row_rstd, t + 1)
                dve.tensor_scalar(row_t[t % BT], row_t[t % BT], mv2[:, t, 0:1], std2[:, 2, t:t + 1],
                                  ALU.subtract, ALU.mult).then_inc(row_ln, 1)

            def top_sum(hf):
                dve.wait_ge(part_sum, hf + 1)
                for c in range(KD):
                    dve.wait_ge(t1_mm, hf * KD + c + 1)
                    dve.tensor_tensor(h1_T[:, c, :], ps[:, 4 + c, :], part[hf][:, c, 0, :], ALU.add).then_inc(t1_sum, 1)

            def sup_tile(t, par, first=False, last=False):
                strengths(t, par)
                for z in range(2):
                    f, q = 2 * t + z, 2 * par + z
                    reciprocals(f, q)
                    if not (first and z == 0):
                        vanished(f - 1, (q - 1) % 4)
                    tile_of[0] = t
                    sums(f, q)
                    if last and z:
                        amplitude_sum(0, 0)
                    if not (first and z == 0):
                        tile_of[1] = t if z else t - 1
                        total(f - 1, (q - 1) % 4)
                    if not (last and z):
                        magnitudes(f + 1, (q + 1) % 4)
                    if z == 0 and not first:
                        norm_eps(t - 1, 1 - par)
                        norm_rows(t - 1, 1 - par)

            magnitudes(0, 0)
            sup_tile(0, 0, first=True)
            sup_tile(1, 1)
            with dve.Fori(1, T // 2 - 1) as i:
                sup_tile(2 * i, 0)
                sup_tile(2 * i + 1, 1)
            sup_tile(T - 2, 0)
            sup_tile(T - 1, 1, last=True)
            amplitude_sum(0, 1)
            vanished(STEPS - 1, 3)
            amplitude_sum(0, 2)
            amplitude_sum(0, 3)
            tile_of[1] = T - 1
            total(STEPS - 1, 3)
            norm_eps(T - 1, 1)
            norm_rows(T - 1, 1)
            row_stats(0)
            row_stats(1)
            row_norm(0)
            row_norm(1)
            row_stats(2)
            row_stats(3)
            row_norm(2)
            row_norm(3)
            amplitude_sum(1, 0)
            amplitude_sum(1, 1)
            amplitude_sum(1, 2)
            amplitude_sum(1, 3)
            top_sum(0)
            row_stats(4)
            row_stats(5)
            row_norm(4)
            row_norm(5)
            row_stats(6)
            row_stats(7)
            row_norm(6)
            row_norm(7)
            top_sum(1)

        @block.tensor
        def _(pe):
            pe.sem_inc(w_used, CREDIT_W)
            with pe.Fori(0, HALVES) as half:
                for e in range(2):
                    def it(n):
                        return half * (2 * n) + e * n

                    def unit(u, s):
                        pe.wait_ge(split_done, stream_pos(half, e, u, not isinstance(u, int) and late[0]) + 1)
                        return w_hi[s], w_lo[s]

                    late = [False]
                    with pe.Fori(0, HC // 2) as hp:
                        for par in range(2):
                            if par == 0:
                                pe.wait_ge(s_evac, it(OC) + 1)
                            pe.wait_ge(h_evac, it(4 * HC) + hp * 8 + par * 4 + 4)
                            for j in range(8):
                                wh, wl = unit(hp * 16 + par * 8 + j, j % 2)
                                if e == 0 and par == 0:
                                    pe.wait_ge(x_split, j + 1)
                                for kk in range(2):
                                    k = 2 * j + kk
                                    for bt in range(BT):
                                        b = slice(bt * P, bt * P + P)
                                        w = slice(kk * 512, kk * 512 + 512)
                                        last = mm3(pe, ps[:, par * 4 + bt, :], x_hi[:, k, b], x_lo[:, k, b],
                                                   wh[:, w], wl[:, w], k == 0, k == KX - 1)
                                last.then_inc(w_used, 1)
                    def turn(k):
                        if k >= 4:
                            pe.wait_ge(gelu_done, it(KH) + k - 3)
                        for bt in range(BT):
                            last = pe.transpose(ps[:, 4 + k % 4, bt * P:bt * P + P], h[:, bt, k * P:k * P + P], ident[:, :])
                        last.then_inc(tr_done, 1)

                    pe.wait_ge(h_evac, it(4 * HC) + CREDIT_H + 12)
                    for j in range(U_TOP):
                        if j == U_TOP - 1:
                            pe.wait_ge(ln_done, it(BT) + BT)
                            pe.wait_ge(consts_in, 32)
                            for k in range(4):
                                turn(k)
                        wh, wl = unit(U_ENC1 + j, j % 2)
                        for kk in range(2):
                            k = e * 8 + 2 * j + kk
                            for c in range(4):
                                w = slice(kk * 512 + c * P, kk * 512 + c * P + P)
                                last = mm3(pe, ps[:, c, :], wh[:, w], wl[:, w], x_hi[:, k, :], x_lo[:, k, :],
                                           2 * j + kk == 0, 2 * j + kk == 7)
                        last.then_inc(w_used, 1)

                    def second(oc, q, first=False):
                        for v in range(2):
                            wh, wl = unit(U_ENC1 + U_TOP + 2 * oc + v, v)
                            for kk in range(8):
                                k = v * 8 + kk
                                if first:
                                    pe.wait_ge(hT_done, it(KH) + k + 1)
                                w = slice(kk * P, kk * P + P)
                                last = mm3(pe, ps[:, q, :], wh[:, w], wl[:, w], hT_hi[:, k, :], hT_lo[:, k, :],
                                           k == 0, k == KH - 1)
                                if kk == 7:
                                    last.then_inc(w_used, 1)
                                if first and k + 4 < KH:
                                    turn(k + 4)

                    for oc in range(8):
                        if oc < 4:
                            pe.wait_ge(top_evac, it(4) + oc + 1)
                        else:
                            pe.wait_ge(s_evac, it(OC) + oc - 2)
                        second(oc, oc % 4, oc == 0)
                    late = [True]
                    with pe.Fori(2, OC // 4) as og:
                        for q in range(4):
                            pe.wait_ge(s_evac, it(OC) + og * 4 + q - 2)
                            second(og * 4 + q, q)

            pe.sem_inc(sc_mm, 8)

            def project(g, t, c, par):
                for a, m in enumerate(ORDER):
                    pe.wait_ge(qk_low, 4 * g + a + 1)
                    if isinstance(g, int) and g == 0:
                        pe.wait_ge(s_evac, 1 + 4 * OC)
                    e = m % 2
                    for kd in range(KD):
                        if c == 0 and kd % 2 == 0:
                            pe.wait_ge(split_done, 4 * t + U_A + 2 * e + kd // 2 + 1)
                        w = slice(c * P, c * P + P)
                        last = mm3(pe, ps[:, a, :], x_hi[:, 4 * m + kd, w], x_lo[:, 4 * m + kd, w],
                                   s_hi[par][:, e, kd, :], s_lo[par][:, e, kd, :], kd == 0, kd == KD - 1)
                    last.then_inc(qk_mm, 1)

            def scores(g, slot):
                pe.wait_ge(qk_low, 4 + 4 * g + 4)
                pe.wait_ge(neg_done, g + 1)
                for hh in range(2):
                    for sub in range(SUB):
                        idx = hh * SUB + sub
                        out = ps[:, 4 + idx // 2, (idx % 2) * 256:(idx % 2) * 256 + 256]
                        if idx % 2 == 0:
                            pe.wait_ge(sc_masked, 4 * g + idx // 2 + 1)
                        q = [q_t[slot][:, z, hh, sub * P:sub * P + P] for z in range(2)]
                        k = [k_t[slot][:, z, hh, :, sub * P:sub * P + P] for z in range(2)]
                        last = mm3(pe, out, q[0], q[1], k[0], k[1], True, True)
                        if idx % 2 == 1:
                            last.then_inc(sc_mm, 1)

            def score_tile(t, par, first=False):
                for c in range(KD):
                    project(t * 4 + c, t, c, par)
                    if not (first and c == 0):
                        scores(t * 4 + c - 1, (c - 1) % 2)

            score_tile(0, 0, first=True)
            with pe.Fori(0, 3) as i:
                score_tile(2 * i + 1, 1)
                score_tile(2 * i + 2, 0)
            score_tile(7, 1)
            scores(CH - 1, 1)

            pe.sem_inc(av_mm, 2)

            def values(t, sub):
                first = isinstance(t, int)
                q = t * 4 + sub
                for e in range(2):
                    b = sub % 2 * 2 + e
                    if sub >= 2:
                        pe.wait_ge(v_done, 2 * q + e - 3)
                    elif first:
                        pe.wait_ge(qk_low, 4 + 4 * CH)
                    else:
                        pe.wait_ge(wo_evac, t * 8 + b - 3)
                    for kd in range(KD):
                        if sub == 0 and kd % 2 == 0:
                            if first:
                                pe.wait_ge(split_done, U_B + RAW + 2 * e + kd // 2 + 1)
                            else:
                                pe.wait_ge(split_done, t * RAW + U_B + U_X + 2 * e + kd // 2 + 1)
                        x = slice(sub * P, sub * P + P)
                        last = mm3(pe, ps[:, b, :], s_hi[0][:, e, kd, x], s_lo[0][:, e, kd, x],
                                   x_hi[:, 4 * e + kd, :], x_lo[:, 4 * e + kd, :], kd == 0, kd == KD - 1)
                    last.then_inc(v_mm, 1)

            def attend(t, sub):
                first = isinstance(t, int)
                q = t * 4 + sub
                if first and sub < 2:
                    pe.wait_ge(sc_masked, 4 + 4 * CH)
                else:
                    pe.wait_ge(o_low, 4 * q - 4)
                pe.wait_ge(v_done, 2 * q + 2)
                pe.wait_ge(wt_done, q + 1)
                for hd in range(H):
                    last = pe.matmul(ps[:, 4 + sub % 2 * 2 + hd // 4, hd % 4 * P:hd % 4 * P + P],
                                     v_t[sub % 2][:, hd, :, :].rearrange("p e d -> p (e d)"), wt[sub % 2][:, hd, :], start=True, stop=True)
                last.then_inc(av_mm, 1)

            def output(t, j, x):
                e, c = j // 4, j % 4
                w = slice(c * P, c * P + P)
                for kd in range(KD):
                    k = 8 + 4 * e + kd
                    last = mm3(pe, ps[:, c, x], x_hi[:, k, w], x_lo[:, k, w], o_hi[:, e, kd, x], o_lo[:, e, kd, x],
                               kd == 0, kd == KD - 1)
                return last

            def outputs(t):
                pe.wait_ge(o_low, t * 16 + 8)
                if isinstance(t, int):
                    pe.wait_ge(split_done, U_B + RAW + U_X)
                for j in range(4):
                    output(t, j, slice(0, 256))
                for j in range(8):
                    if j % 4 == 0:
                        pe.wait_ge(o_low, t * 16 + 14 + j // 2)
                    if j >= 4:
                        pe.wait_ge(wo_evac, t * 8 + j - 3)
                    output(t, j, slice(256, 512) if j < 4 else slice(0, 512)).then_inc(wo_mm, 1)

            def value_tile(t):
                values(t, 0)
                for sub in range(1, SUB):
                    values(t, sub)
                    attend(t, sub - 1)
                attend(t, 3)
                outputs(t)

            value_tile(0)
            with pe.Fori(1, T) as t:
                value_tile(t)

            def interfere(t, n):
                first = isinstance(t, int) and t == 0
                w = (int_a, int_b)[n // 2][:, n % 2, :, :, :]
                a = at_t[n % 2]
                if first:
                    pe.wait_ge(int_in[n], 16)
                for e in range(2):
                    b = n % 2 * 2 + e
                    if first and n < 2:
                        pe.wait_ge(wo_evac, 8 * T)
                    else:
                        pe.wait_ge(z_evac, t * 8 + 2 * n + e - 3)
                    pe.wait_ge(neg2, t * 4 + n + 1)
                    for part in range(2):
                        src = part if e else 2 * part
                        for k in range(KD):
                            last = pe.matmul(ps[:, b, :], a[:, src, k, :], w[:, part ^ e, k, :],
                                             start=(part == 0 and k == 0), stop=(part == 1 and k == KD - 1))
                    last.then_inc(z_mm, 1)

            def turn_sup(t, par):
                pe.wait_ge(nrm_b, t * 2 + 2)
                if not (isinstance(t, int) and t == 0):
                    pe.wait_ge(st_evac, t * 2)
                elif t == 0:
                    pe.wait_ge(o_low, 16 * T)
                for e in range(2):
                    for k in range(KD):
                        last = pe.transpose(ps[:, 6 + e, k * P:k * P + P], sup_t[par][:, e, k * P:k * P + P], ident[:, :])
                    last.then_inc(st_mm, 1)

            def sup_tile(t, par):
                for n in range(N):
                    interfere(t, n)
                if not isinstance(t, int) or t >= 2:
                    turn_sup(t - 2, par)

            sup_tile(0, 0)
            sup_tile(1, 1)
            sup_tile(2, 0)
            sup_tile(3, 1)
            with pe.Fori(2, T // 2) as i:
                sup_tile(2 * i, 0)
                sup_tile(2 * i + 1, 1)

            def measure(hf, c, tiles=(0, BT)):
                x = slice(tiles[0] * P, tiles[1] * P)
                g = hf * KD + c
                if g < 2:
                    pe.wait_ge(z_evac, 8 * T - 2 + 2 * g)
                else:
                    pe.wait_ge(me_sq, 2 * g - 2)
                pe.wait_ge(st_evac, hf * T + 2 * tiles[1])
                for e in (1, 0):
                    for src in range(2):
                        if g == 0 and e == 0 and src == 1:
                            pe.wait_ge(neg3, 1)
                        w = meas_neg if src and not e else meas[:, src ^ e, :, :]
                        for k in range(KD):
                            last = pe.matmul(ps[:, c % 2 * 2 + e, x], w[:, k, c * P:c * P + P], sup_T[:, src, k, hf * HB:hf * HB + HB][:, x],
                                             start=(src == 0 and k == 0), stop=(src == 1 and k == KD - 1))
                if tiles[1] == BT:
                    last.then_inc(me_mm, 1)

            def post(t):
                hf, b = t // BT, 4 + t % 2
                pe.wait_ge(fin_in["post"], 16)
                pe.wait_ge(amp, (hf + 1) * KD)
                if t in (4, 5):
                    pe.wait_ge(t1_sum, t - 3)
                elif t >= 2:
                    pe.wait_ge(row_in, t - 1)
                for k in range(KD):
                    last = pe.matmul(ps[:, b, :], amp_T[:, hf, k, t % BT * P:t % BT * P + P], post_wt[:, k, :],
                                     start=(k == 0), stop=(k == KD - 1))
                last.then_inc(row_mm, 1)

            def turn_row(t):
                pe.wait_ge(row_ln, t + 1)
                if t < 2:
                    pe.wait_ge(st_evac, 2 * T)
                elif t in (4, 5):
                    pe.wait_ge(t1_sum, t - 1)
                else:
                    pe.wait_ge(z_gelu, (t - 1) * KD)
                for k in range(KD):
                    last = pe.transpose(ps[:, 6 + t % 2, k * P:k * P + P], row_t[t % BT][:, k * P:k * P + P], ident[:, :])
                last.then_inc(row_tr, 1)

            def top_1(hf):
                pe.wait_ge(fin_in["topz"], 16)
                pe.wait_ge(z_gelu, (hf + 1) * BT * KD)
                if hf:
                    pe.wait_ge(t2_relu, 2)
                    pe.wait_ge(y_done, 1)
                for c in range(KD):
                    for k in range(KD):
                        last = pe.matmul(ps[:, 4 + c, :], topz[:, k, c * P:c * P + P], z_out[hf][:, k, :],
                                         start=(k == 0), stop=(k == KD - 1))
                    last.then_inc(t1_mm, 1)

            def top_2(hf):
                pe.wait_ge(fin_in["top2"], 16)
                pe.wait_ge(t1_relu, (hf + 1) * KD)
                if hf == 0:
                    pe.wait_ge(row_in, T)
                for c in range(2):
                    for k in range(KD):
                        last = pe.matmul(ps[:, 4 + c, :], top2_wt[:, k, c * P:c * P + P], h1_T[:, k, :],
                                         start=(k == 0), stop=(k == KD - 1))
                    last.then_inc(t2_mm, 1)

            def top_3(hf):
                pe.wait_ge(t2_relu, (hf + 1) * 2)
                if hf == 0:
                    pe.wait_ge(z_gelu, (T - 1) * KD)
                for k in range(2):
                    last = pe.matmul(ps[0:1, 6, :], col(C_W3 + k), h2_T[:, k, :], start=(k == 0), stop=(k == 1))
                last.then_inc(y_mm, 1)

            pe.wait_ge(fin_in["meas"], 16)
            measure(0, 0)
            measure(0, 1)
            measure(0, 2)
            turn_sup(T - 2, 0)
            measure(0, 3)
            measure(1, 0, (0, BT - 1))
            post(0)
            post(1)
            turn_sup(T - 1, 1)
            measure(1, 0, (BT - 1, BT))
            post(2)
            post(3)
            turn_row(0)
            turn_row(1)
            measure(1, 1)
            turn_row(2)
            turn_row(3)
            measure(1, 2)
            measure(1, 3)
            top_1(0)
            for t in range(BT, T):
                post(t)
            top_2(0)
            for t in range(BT, T):
                turn_row(t)
            top_3(0)
            top_1(1)
            top_2(1)
            top_3(1)


def swap_heads(w):
    return w.reshape(KD, 2, HD, -1)[:, ::-1].reshape(w.shape)


def chunks(w):
    return w.reshape(-1, P, w.shape[1]).transpose(1, 0, 2).reshape(P, -1)


def pair(wr, wi):
    import numpy as np
    return np.concatenate([chunks(wr.T), chunks(wi.T)], 1)


def lay_out(i, np):
    x = i["r_x"]
    xu = np.empty((4, U_X, P, UNIT), x.dtype)
    for hf in range(2):
        xu[hf] = x[hf * HB:(hf + 1) * HB].T.reshape(U_X, 2, P, HB).transpose(0, 2, 1, 3).reshape(U_X, P, UNIT)
    for m, n in enumerate(("Wq_r", "Wq_i", "Wk_r", "Wk_i", "Wv_r", "Wv_i", "Wo_r", "Wo_i")):
        w = i["L0_rec_" + n]
        if m in (Q_I, K_I):
            w = swap_heads(w)
        xu[2 + m // 4, 2 * (m % 4):2 * (m % 4) + 2] = w.T.reshape(2, 2, P, D).transpose(0, 2, 1, 3).reshape(2, P, UNIT)
    wu = np.empty((2, U_PASS, P, UNIT), x.dtype)
    top = i["W_top1"][D:].reshape(2, U_TOP, 2, P, 512).transpose(0, 1, 3, 2, 4).reshape(2, U_TOP, P, UNIT)
    for e, n in enumerate(("er", "ei")):
        w1, w2 = i[f"L0_rec_{n}_W1"], i[f"L0_rec_{n}_W2"]
        wu[e, :U_ENC1] = w1.T.reshape(KX // 2, 2, P, HC, 512).transpose(3, 0, 2, 1, 4).reshape(U_ENC1, P, UNIT)
        wu[e, U_ENC1:U_ENC1 + U_TOP] = top[e]
        wu[e, U_ENC1 + U_TOP:] = w2.T.reshape(2, 8, P, OC, P).transpose(3, 0, 2, 1, 4).reshape(U_ENC2, P, UNIT)
    b1 = np.stack([i["L0_rec_er_b1"], i["L0_rec_ei_b1"]])
    c = []
    for n in ("er", "ei"):
        for v in ("g1", "be1", "b2"):
            c.append(i[f"L0_rec_{n}_{v}"].reshape(-1, P).T)
    for n in ("bq_r", "bq_i", "bk_r", "bk_i", "bv_r", "bv_i", "bo_r", "bo_i"):
        c.append((swap_heads(i["L0_rec_" + n]) if n in ("bq_i", "bk_i") else i["L0_rec_" + n]).reshape(-1, P).T)
    c += [i["b_top1"].reshape(-1, P).T, i["b_top2"].reshape(-1, P).T, i["W_top3"].reshape(-1, P).T]
    c += [i["L0_rec_post_g"].reshape(-1, P).T, i["L0_rec_post_be"].reshape(-1, P).T]
    cols = np.ascontiguousarray(np.concatenate(c, 1))
    eye = np.eye(P, dtype=np.float32)
    return {"x_units": xu, "w_units": wu, "b1": b1, "cols": cols, "eye": eye, "mask_d": np.tile(np.eye(32, dtype=np.float32), (4, 1)),
            "bv": np.concatenate([i["L0_rec_bv_r"], i["L0_rec_bv_i"]]).reshape(1, 2 * D),
            "ids": np.ascontiguousarray(i["ids"].reshape(T, P, N).transpose(1, 0, 2).reshape(P, T * N)),
            "int_w": np.stack([pair(i["L0_rec_int_Wr"][n], i["L0_rec_int_Wi"][n]) for n in range(N)]),
            "meas_w": pair(i["L0_rec_meas_Mr"], i["L0_rec_meas_Mi"]),
            "post_w": chunks(i["L0_rec_post_W"].T), "post_b": i["L0_rec_post_b"].reshape(1, D),
            "topz_w": chunks(i["W_top1"][:D]), "top2_w": chunks(i["W_top2"])}


def kernel(**inputs):
    import numpy as np
    import concourse.bacc as bacc
    from concourse.bass_utils import run_bass_kernel_spmd

    nc = bacc.Bacc("TRN2", target_bir_lowering=False, num_devices=1)
    inputs = {k: np.asarray(v) for k, v in inputs.items()}
    laid = lay_out(inputs, np)
    arrays = {f"in_{name}": a for name, a in laid.items()}
    arrays.update({f"in_tbl_{n}": inputs[f"tbl_{n}"] for n in range(N)})
    aps = {name[3:]: nc.dram_tensor(name, a.shape, mybir.dt.from_np(a.dtype), kind="ExternalInput").ap() for name, a in arrays.items()}
    tbls = [aps.pop(f"tbl_{n}") for n in range(N)]
    s_T = nc.dram_tensor("s_T", (2, T, P, KD, N, P), F32).ap()
    top_part = nc.dram_tensor("top_part", (2, KD, P, B), F32).ap()
    at_T = nc.dram_tensor("at_T", (T, N, P, 2, KD, P), F32).ap()
    y = nc.dram_tensor("out_y", (1, B), F32, kind="ExternalOutput").ap()
    build(nc, **aps, tbls=tbls, s_T=s_T, top_part=top_part, at_T=at_T, y=y)
    r = run_bass_kernel_spmd(nc, [arrays], core_ids=[0])
    return r.results[0]["out_y"].reshape(B, 1)
```
